# Optimizing a Trainium2 kernel written in Bass

```python
import numpy as np
import jax
import jax.numpy as jnp

def _softmax(x, axis=-1):
    return jax.nn.softmax(x, axis=axis)

def _gelu(x):
    return jax.nn.gelu(x, approximate=True)

def _silu(x):
    return jax.nn.silu(x)

def _sigmoid(x):
    return jax.nn.sigmoid(x)

def _layernorm(x, axis=-1, eps=1e-05):
    m = jnp.mean(x, axis=axis, keepdims=True)
    v = jnp.var(x, axis=axis, keepdims=True)
    return (x - m) / jnp.sqrt(v + eps)

def _scatter_add(tgt, idx, src, axis=0):
    return tgt.at[idx].add(src)

def _segment_sum(src, seg, n):
    return jax.ops.segment_sum(src, seg, n)
kernel_name = 'mk_xattn_seq_d1_seqx_r2_7e8176'

def setup_inputs(seed: int=0):
    np.random.seed(seed)
    _w = jnp.asarray

    def _rec_inputs():
        import jax
        import jax.numpy as jnp
        _rk = jax.random.key(seed)
        x = -0.000125 + 0.9999 * jax.random.normal(jax.random.fold_in(_rk, 1), (16, 100, 512), jnp.float32)
        _lenS = 100 - jax.random.randint(jax.random.fold_in(_rk, 7), (16,), 0, max(1, 100 // 4) + 1, jnp.int32)
        _lenS2 = 722 - jax.random.randint(jax.random.fold_in(_rk, 8), (16,), 0, max(1, 722 // 4) + 1, jnp.int32)
        _ctx_512P = jax.random.normal(jax.random.fold_in(_rk, 11), (16, 16, 256), jnp.float32)
        _ctx_512c = jax.random.dirichlet(jax.random.fold_in(_rk, 511), 0.3 * jnp.ones((16,), jnp.float32), (16, 722))
        _ctx_512t = jnp.einsum('bsk,bkd->bsd', _ctx_512c, _ctx_512P)
        _ctx_512t = _ctx_512t * jax.lax.rsqrt(jnp.mean(jnp.square(_ctx_512t)) + 1e-12) * 0.953939
        ctx_512 = 0.000227908 + 0.99994 * (_ctx_512t + 0.3 * jax.random.normal(jax.random.fold_in(_rk, 611), (16, 722, 256), jnp.float32))
        return (x, ctx_512)
    x, ctx_512 = _rec_inputs()

    def _L0_xattn_setup():
        import jax, jax.numpy as jnp
        import numpy as np
        B, T, E = (8, 2048, 512)
        M, L = (128, 256)
        EPS = 1e-06
        key = jax.random.key(seed)
        ks = jax.random.split(key, 5)
        return {'emb': jax.random.normal(ks[0], (B, T, E), dtype=jnp.float32), 'latent': jax.random.normal(ks[1], (B, M, L), dtype=jnp.float32), 'Wq': jax.random.normal(ks[2], (E, E), dtype=jnp.float32) * (1.0 / np.sqrt(E)), 'bq': jnp.zeros((E,), dtype=jnp.float32), 'Wk': jax.random.normal(ks[3], (L, E), dtype=jnp.float32) * (1.0 / np.sqrt(L)), 'bk': jnp.zeros((E,), dtype=jnp.float32), 'Wv': jax.random.normal(ks[4], (L, E), dtype=jnp.float32) * (1.0 / np.sqrt(L)), 'bv': jnp.zeros((E,), dtype=jnp.float32), 'gamma': jnp.ones((E,), dtype=jnp.float32), 'beta': jnp.zeros((E,), dtype=jnp.float32)}
    _L0_xattn_all = _L0_xattn_setup()
    _L0_xattn_in = {k: v for k, v in _L0_xattn_all.items() if k in ('Wq', 'bq', 'Wk', 'bk', 'Wv', 'bv', 'gamma', 'beta')}
    del _L0_xattn_all
    return {'x': x, 'ctx_512': ctx_512, 'L0_xattn_Wq': _L0_xattn_in['Wq'], 'L0_xattn_bq': _L0_xattn_in['bq'], 'L0_xattn_Wk': _L0_xattn_in['Wk'], 'L0_xattn_bk': _L0_xattn_in['bk'], 'L0_xattn_Wv': _L0_xattn_in['Wv'], 'L0_xattn_bv': _L0_xattn_in['bv'], 'L0_xattn_gamma': _L0_xattn_in['gamma'], 'L0_xattn_beta': _L0_xattn_in['beta']}

def reference(x, ctx_512, L0_xattn_Wq, L0_xattn_bq, L0_xattn_Wk, L0_xattn_bk, L0_xattn_Wv, L0_xattn_bv, L0_xattn_gamma, L0_xattn_beta):
    import jax
    import jax.numpy as jnp

    def _L0_xattn_ref(emb, latent, Wq, bq, Wk, bk, Wv, bv, gamma, beta):
        import jax, jax.numpy as jnp
        import numpy as np
        B, T, E = (8, 2048, 512)
        M, L = (128, 256)
        EPS = 1e-06
        q = jnp.einsum('bte,ef->btf', emb, Wq) + bq
        k = jnp.einsum('bml,le->bme', latent, Wk) + bk
        v = jnp.einsum('bml,le->bme', latent, Wv) + bv
        scale = 1.0 / jnp.sqrt(jnp.asarray(E, dtype=q.dtype))
        w = jnp.einsum('bte,bme->btm', q, k) * scale
        w = jax.nn.softmax(w, axis=1)
        pred = jnp.einsum('btm,bme->bte', w, v)
        x = pred + emb
        mu = jnp.mean(x, axis=-1, keepdims=True)
        var = jnp.var(x, axis=-1, keepdims=True)
        return (x - mu) * jax.lax.rsqrt(var + EPS) * gamma + beta
    x = _L0_xattn_ref(x, ctx_512, L0_xattn_Wq, L0_xattn_bq, L0_xattn_Wk, L0_xattn_bk, L0_xattn_Wv, L0_xattn_bv, L0_xattn_gamma, L0_xattn_beta)
    return x

_drawn_inputs = setup_inputs


def setup_inputs(seed=0):
    import zlib

    import numpy as np

    out = dict(_drawn_inputs(seed))
    spreads = {'L0_xattn_bq': (0.0, 0.1),
     'L0_xattn_bk': (0.0, 0.1),
     'L0_xattn_bv': (0.0, 0.1),
     'L0_xattn_gamma': (1.0, 0.2),
     'L0_xattn_beta': (0.0, 0.1)}
    factors = {}
    for name, (base, spread) in spreads.items():
        noise = np.random.default_rng([zlib.crc32(name.encode()), seed]).standard_normal(out[name].shape)
        drawn = base * np.exp(spread * noise) if base else spread * noise
        out[name] = jnp.asarray(drawn.astype(out[name].dtype))
    for name, factor in factors.items():
        out[name] = (out[name] * factor).astype(out[name].dtype)
    return out
```

```python
from contextlib import ExitStack

import concourse.bass as bass
from concourse import mybir

ALU = mybir.AluOpType
ACT = mybir.ActivationFunctionType
AX = mybir.AxisListType
F32 = mybir.dt.float32
F32R = mybir.dt.float32r

P = 128
EPS = 1e-6


def xattn(nc, xT, x, ctxT, ctx, WqT, WkT, bq, bk, Wv, bv, gamma, beta, out):
    B, T, E = x.shape
    _, M, L = ctx.shape
    EC, LC = E // P, L // P
    MC = 6
    MP = -(-M // MC)
    ML = M - (MC - 1) * MP
    HALF = MC // 2
    GB = 4
    NG = B // GB
    GT = GB * T
    SCALE = float(E) ** -0.5
    assert HALF * T <= 512 and GT <= 512 and NG % 2 == 0 and B % 2 == 0

    with ExitStack() as stack:
        def sb(name, shape, dt=F32):
            return stack.enter_context(nc.sbuf_tensor(name, shape, dt))

        def ps(name, shape):
            return stack.enter_context(nc.psum_tensor(name, shape, F32))

        def sem(name):
            return stack.enter_context(nc.semaphore(name))

        wqT = sb("wqT", [P, EC, E])
        wkT = sb("wkT", [P, EC, L + 1])
        bk_in = sb("bk_in", [P, EC])
        bk_wide = sb("bk_wide", [P, EC, P])
        bq_col = sb("bq_col", [P, EC])
        W_hi = sb("W_hi", [P, EC, L], F32R)
        W_lo = sb("W_lo", [P, EC, L], F32R)
        u_col = sb("u_col", [P, EC])
        g_bias = sb("g_bias", [P, LC])
        c_bias = sb("c_bias", [P, 1])
        wv_in = sb("wv_in", [P, LC, E])
        Wv_hi = sb("Wv_hi", [P, LC, E], F32R)
        Wv_lo = sb("Wv_lo", [P, LC, E], F32R)
        bv_rows = sb("bv_rows", [T, E])
        gamma_rows = sb("gamma_rows", [T, E])
        beta_rows = sb("beta_rows", [T, E])
        ones = sb("ones", [P, P])
        mask = sb("mask", [P, MC])
        neg_half = sb("neg_half", [T, 1])
        xT_in = sb("xT_in", [P, 2, EC, GT])
        xT_hi = sb("xT_hi", [P, 2, EC, GT], F32R)
        xT_lo = sb("xT_lo", [P, 2, EC, GT], F32R)
        xu = sb("xu", [P, 2, EC, GT])
        G = sb("G", [P, LC, B * T])
        c_rows = sb("c_rows", [P, B * T])
        ctxT_in = sb("ctxT_in", [P, 2, LC, M])
        ctx_in = sb("ctx_in", [P, 2, MC, L])
        x_in = sb("x_in", [T, 2, E])
        scores = sb("scores", [P, 2, MC * T])
        negmax = sb("negmax", [P, 2, MC])
        expo = sb("expo", [P, 2, MC * T])
        expsum = sb("expsum", [P, 2, MC])
        rall = sb("rall", [P, 2, MC])
        rinv = sb("rinv", [P, 2, MC])
        prob = sb("prob", [P, 2, MC * T])
        probsum = sb("probsum", [P, 2, T])
        U_hi = sb("U_hi", [P, 2, LC * T], F32R)
        U_lo = sb("U_lo", [P, 2, LC * T], F32R)
        wsum = sb("wsum", [T, 2])
        bvw = sb("bvw", [T, 2, E])
        resid = sb("resid", [T, 2, E])
        y = sb("y", [T, 2, E])
        stats = sb("stats", [T, 2, 6])
        meanvar = sb("meanvar", [T, 2, 2])
        vareps = sb("vareps", [T, 2])
        rstd = sb("rstd", [T, 2])
        centred = sb("centred", [T, 2, E])
        scaled = sb("scaled", [T, 2, E])
        result = sb("result", [T, 2, E])

        ps_S = ps("ps_S", [P, 2, 512])
        ps_U = ps("ps_U", [P, 2, 512])
        ps_Y = ps("ps_Y", [P, 2, 512])
        ps_w = ps("ps_w", [P, 512])
        ps_c = ps("ps_c", [P, 512])

        wk_in = sem("wk_in")
        wq_in = [sem(f"wq_in{c}") for c in range(EC)]
        small_in = sem("small_in")
        xT_loaded = [sem(f"xT_loaded{q}") for q in range(2)]
        wv_loaded = sem("wv_loaded")
        rows_in = sem("rows_in")
        ctxT_loaded = [sem(f"ctxT_loaded{q}") for q in range(2)]
        ctx_loaded = [sem(f"ctx_loaded{q}") for q in range(2)]
        x_loaded = [sem(f"x_loaded{q}") for q in range(2)]
        out_stored = [sem(f"out_stored{q}") for q in range(2)]
        consts_set = sem("consts_set")
        bkcol_set = sem("bkcol_set")
        scores_zeroed = sem("scores_zeroed")
        W_summed = sem("W_summed")
        gbias_summed = sem("gbias_summed")
        cbias_summed = sem("cbias_summed")
        Whi_set = sem("Whi_set")
        Wlo_set = sem("Wlo_set")
        u_set = sem("u_set")
        gbias_set = sem("gbias_set")
        cbias_set = sem("cbias_set")
        Wvhi_set = sem("Wvhi_set")
        Wvlo_set = sem("Wvlo_set")
        mask_set = sem("mask_set")
        xThi_set = sem("xThi_set")
        xTlo_set = sem("xTlo_set")
        xu_step = sem("xu_step")
        G_summed = sem("G_summed")
        c_summed = sem("c_summed")
        G_set = sem("G_set")
        c_set = sem("c_set")
        S_done = sem("S_done")
        S_read = sem("S_read")
        negmax_set = sem("negmax_set")
        exp_done = sem("exp_done")
        rall_set = sem("rall_set")
        rinv_set = sem("rinv_set")
        prob_set = sem("prob_set")
        probsum_set = sem("probsum_set")
        U_done = sem("U_done")
        Uhi_set = sem("Uhi_set")
        Ulo_set = sem("Ulo_set")
        wsum_done = sem("wsum_done")
        wsum_set = sem("wsum_set")
        bvw_set = sem("bvw_set")
        resid_set = sem("resid_set")
        Y_done = sem("Y_done")
        y_set = sem("y_set")
        stats_set = sem("stats_set")
        meanvar_set = sem("meanvar_set")
        vareps_set = sem("vareps_set")
        rstd_set = sem("rstd_set")
        centred_set = sem("centred_set")
        scaled_set = sem("scaled_set")
        result_set = sem("result_set")

        def rows(c):
            return ML if c == MC - 1 else MP

        def ps_scores(c):
            return ps_S[:, c // HALF, (c % HALF) * T:(c % HALF + 1) * T]

        def split_chunks(ap):
            return ap.rearrange("p (b c t) -> p b c t", b=2, t=T)

        block = stack.enter_context(nc.Block())

        @block.sync
        def _(sp):
            sp.dma_start(wkT[:, :, 0:L], WkT.rearrange("(p c) l -> p c l", c=EC)).then_inc(wk_in, 16)
            for c in range(EC):
                sp.dma_start(wqT[:, c, :], WqT.rearrange("(p c) e -> p c e", c=EC)[:, c, :]).then_inc(wq_in[c], 16)

            def load_group(g):
                if g >= 2:
                    sp.wait_ge(xThi_set, g - 1)
                    sp.wait_ge(xTlo_set, g - 1)
                    sp.wait_ge(xu_step, EC * (g - 1))
                sp.dma_start(xT_in[:, g % 2, :, :], xT[g].rearrange("(c p) t -> p c t", p=P)).then_inc(xT_loaded[g % 2], 16)

            def load_ctxT(b, q):
                sp.dma_start(ctxT_in[:, q, :, :], ctxT[b].rearrange("(c p) m -> p c m", p=P)).then_inc(ctxT_loaded[q], 16)

            def load_ctx(b, q):
                full = (MC - 1) * MP
                sp.dma_start(ctx_in[0:MP, q, 0:MC - 1, :],
                             ctx[b, 0:full, :].rearrange("(c p) l -> p c l", p=MP)).then_inc(ctx_loaded[q], 16)
                sp.dma_start(ctx_in[0:ML, q, MC - 1, :], ctx[b, full:M, :]).then_inc(ctx_loaded[q], 16)

            def load_x(b, q):
                sp.dma_start(x_in[:, q, :], x[b, :, :]).then_inc(x_loaded[q], 16)

            load_group(0)
            load_group(1)
            load_ctxT(0, 0)
            load_group(2)
            load_ctx(0, 0)
            load_group(3)
            sp.dma_start(wv_in[:, :, :], Wv.rearrange("(c p) e -> p c e", p=P)).then_inc(wv_loaded, 16)
            load_x(0, 0)
            load_ctxT(1, 1)
            load_ctx(1, 1)
            load_x(1, 1)
            with sp.Fori(2, B - 1, 2) as b0:
                for q in range(2):
                    b = b0 + q
                    sp.wait_ge(S_done, b - 1)
                    load_ctxT(b, q)
                    sp.wait_ge(U_done, b - 1)
                    load_ctx(b, q)
                    sp.wait_ge(resid_set, b - 1)
                    load_x(b, q)

        @block.tensor
        def _(pe):
            banks = [ps_U[:, 0, :], ps_U[:, 1, :], ps_Y[:, 0, :], ps_Y[:, 1, :]]
            pe.wait_ge(wk_in, 16)
            pe.wait_ge(bkcol_set, 1)
            for f in range(EC):
                pe.wait_ge(wq_in[f], 16)
                for e in range(EC):
                    last = nc.tensor.matmul(banks[e][:, 0:L + 1], wqT[:, f, e * P:(e + 1) * P], wkT[:, f, :],
                                            start=(f == 0), stop=(f == EC - 1))
            last.then_inc(W_summed, 1)
            pe.wait_ge(small_in, 32)
            for c in range(LC):
                for f in range(EC):
                    last = nc.tensor.matmul(ps_w[:, c:c + 1], wkT[:, f, c * P:(c + 1) * P], bq_col[:, f:f + 1],
                                            start=(f == 0), stop=(f == EC - 1))
            last.then_inc(gbias_summed, 1)
            pe.wait_ge(bkcol_set, 2)
            for f in range(EC):
                last = nc.tensor.matmul(ps_c[:, 0:1], bk_wide[:, f, :], bq_col[:, f:f + 1],
                                        start=(f == 0), stop=(f == EC - 1))
            last.then_inc(cbias_summed, 1)

            pe.wait_ge(Whi_set, EC)
            pe.wait_ge(Wlo_set, EC)
            for g in range(NG):
                q = g % 2
                bank = ps_Y if q == 0 else ps_U
                pe.wait_ge(xThi_set, g + 1)
                pe.wait_ge(xTlo_set, g + 1)
                if g >= 2:
                    pe.wait_ge(G_set, g - 1)
                for c in range(LC):
                    n = 0
                    for wpart, xpart in ((W_hi, xT_hi), (W_hi, xT_lo), (W_lo, xT_hi)):
                        for e in range(EC):
                            last = nc.tensor.matmul(bank[:, c, 0:GT], wpart[:, e, c * P:(c + 1) * P],
                                                    xpart[:, q, e, :], start=(n == 0), stop=(n == 3 * EC - 1))
                            n += 1
                last.then_inc(G_summed, 1)
                pe.wait_ge(xu_step, EC * (g + 1))
                if g >= 1:
                    pe.wait_ge(c_set, g)
                nc.tensor.matmul(ps_c[:, 0:GT], ones[:, :], xu[:, q, EC - 1, :], start=True, stop=True).then_inc(c_summed, 1)

            def scores_of(b, q):
                pe.wait_ge(ctxT_loaded[q], 8 * (b - q) + 16)
                if isinstance(b, int) and b == 0:
                    pe.wait_ge(G_set, NG)
                else:
                    pe.wait_ge(S_read, b)
                for c in range(MC):
                    for l in range(LC):
                        last = nc.tensor.matmul(ps_scores(c)[0:rows(c), :],
                                                ctxT_in[:, q, l, c * MP:c * MP + rows(c)],
                                                G[:, l, bass.ds(b * T, T)], start=(l == 0), stop=(l == LC - 1))
                last.then_inc(S_done, 1)

            def weighted_ctx(b, q, first):
                pe.wait_ge(ctx_loaded[q], 16 * (b - q) + 32)
                pe.wait_ge(prob_set, b + 1)
                if not first:
                    pe.wait_ge(Ulo_set, b - 1)
                for l in range(LC):
                    for c in range(MC):
                        last = nc.tensor.matmul(ps_U[:, q, l * T:(l + 1) * T],
                                                ctx_in[0:rows(c), q, c, l * P:(l + 1) * P],
                                                prob[0:rows(c), q, c * T:(c + 1) * T], start=(c == 0), stop=(c == MC - 1))
                last.then_inc(U_done, 1)

            def weight_sum(b, q):
                pe.wait_ge(probsum_set, b + 1)
                if not (isinstance(b, int) and b == 0):
                    pe.wait_ge(wsum_set, b)
                nc.tensor.matmul(ps_w[0:T, 0:1], probsum[0:MP, q, :], ones[0:MP, 0:1], start=True, stop=True).then_inc(wsum_done, 1)

            def values(b, q, first):
                pe.wait_ge(Uhi_set, b + 1)
                pe.wait_ge(Ulo_set, b + 1)
                if not first:
                    pe.wait_ge(y_set, b - 1)
                n = 0
                for upart, vpart in ((U_hi, Wv_hi), (U_hi, Wv_lo), (U_lo, Wv_hi)):
                    for l in range(LC):
                        last = nc.tensor.matmul(ps_Y[0:T, q, :], upart[:, q, l * T:(l + 1) * T], vpart[:, l, :],
                                                start=(n == 0), stop=(n == 3 * LC - 1))
                        n += 1
                last.then_inc(Y_done, 1)

            scores_of(0, 0)
            scores_of(1, 1)
            weighted_ctx(0, 0, True)
            weight_sum(0, 0)
            pe.wait_ge(Wvhi_set, 1)
            pe.wait_ge(Wvlo_set, 1)
            for b in (2, 3):
                scores_of(b, b % 2)
                values(b - 2, b % 2, True)
                weighted_ctx(b - 1, 1 - b % 2, b == 2)
                weight_sum(b - 1, 1 - b % 2)
            with pe.Fori(4, B - 1, 2) as b0:
                for q in range(2):
                    b = b0 + q
                    scores_of(b, q)
                    values(b - 2, q, False)
                    weighted_ctx(b - 1, 1 - q, False)
                    weight_sum(b - 1, 1 - q)
            values(B - 2, 0, False)
            weighted_ctx(B - 1, 1, False)
            weight_sum(B - 1, 1)
            values(B - 1, 1, False)

        @block.scalar
        def _(act):
            with nc.allow_non_contiguous_dma("small constants"):
                act.dma_start(bk_in[:, :], bk.rearrange("(p c) -> p c", c=EC)).then_inc(small_in, 16)
                act.dma_start(bq_col[:, :], bq.rearrange("(p c) -> p c", c=EC)).then_inc(small_in, 16)
            act.dma_start(bv_rows[:, :], bv.partition_broadcast(T)).then_inc(rows_in, 16)
            act.dma_start(gamma_rows[:, :], gamma.partition_broadcast(T)).then_inc(rows_in, 16)
            act.dma_start(beta_rows[:, :], beta.partition_broadcast(T)).then_inc(rows_in, 16)

            banks = [ps_U[:, 0, :], ps_U[:, 1, :], ps_Y[:, 0, :], ps_Y[:, 1, :]]
            act.wait_ge(W_summed, 1)
            for e in range(EC):
                nc.scalar.activation(W_hi[:, e, :], banks[e][:, 0:L], ACT.Copy, scale=SCALE).then_inc(Whi_set, 1)
            act.wait_ge(gbias_summed, 1)
            nc.scalar.activation(g_bias[:, :], ps_w[:, 0:LC], ACT.Copy, scale=SCALE).then_inc(gbias_set, 1)
            act.wait_ge(cbias_summed, 1)
            nc.scalar.activation(c_bias[:, :], ps_c[:, 0:1], ACT.Copy, scale=SCALE).then_inc(cbias_set, 1)

            def upper_half(g, q):
                act.wait_ge(xT_loaded[q], 8 * (g - q) + 16)
                if g >= 2:
                    act.wait_ge(G_summed, g - 1)
                nc.scalar.activation(xT_hi[:, q, :, :], xT_in[:, q, :, :], ACT.Copy).then_inc(xThi_set, 1)

            def take_group(g, q):
                bank = ps_Y if q == 0 else ps_U
                act.wait_ge(G_summed, g + 1)
                for c in range(LC):
                    last = nc.scalar.activation(G[:, c, g * GT:(g + 1) * GT], bank[:, c, 0:GT], ACT.Identity,
                                                bias=g_bias[:, c:c + 1])
                last.then_inc(G_set, 1)
                act.wait_ge(c_summed, g + 1)
                nc.scalar.activation(c_rows[:, g * GT:(g + 1) * GT], ps_c[:, 0:GT], ACT.Identity,
                                     bias=c_bias[:, 0:1]).then_inc(c_set, 1)

            upper_half(0, 0)
            upper_half(1, 1)
            act.wait_ge(gbias_set, 1)
            act.wait_ge(cbias_set, 1)
            for g in range(NG - 2):
                take_group(g, g % 2)
                upper_half(g + 2, g % 2)
            act.wait_ge(wv_loaded, 16)
            nc.scalar.activation(Wv_hi[:, :, :], wv_in[:, :, :], ACT.Copy).then_inc(Wvhi_set, 1)
            for q in range(2):
                take_group(NG - 2 + q, q)

            def exponentials(b, q, first):
                act.wait_ge(negmax_set, b + 1)
                if not first:
                    act.wait_ge(prob_set, b - 1)
                for c in range(MC):
                    last = nc.scalar.activation(expo[0:MP, q, c * T:(c + 1) * T], scores[0:MP, q, c * T:(c + 1) * T],
                                                ACT.Exp, bias=negmax[0:MP, q, c:c + 1],
                                                accum_out=expsum[0:MP, q, c:c + 1])
                last.then_inc(exp_done, 1)

            def upper_U(b, q, first):
                act.wait_ge(U_done, b + 1)
                if not first:
                    act.wait_ge(Y_done, b - 1)
                nc.scalar.activation(U_hi[:, q, :], ps_U[:, q, 0:LC * T], ACT.Copy).then_inc(Uhi_set, 1)

            def value_bias(b, q, first):
                act.wait_ge(wsum_done, b + 1)
                nc.scalar.activation(wsum[:, q:q + 1], ps_w[0:T, 0:1], ACT.Copy).then_inc(wsum_set, 1)
                act.wait_ge(wsum_set, b + 1)
                if not first:
                    act.wait_ge(resid_set, b - 1)
                nc.scalar.activation(bvw[:, q, :], bv_rows[:, :], ACT.Copy, scale=wsum[:, q:q + 1]).then_inc(bvw_set, 1)

            def scale_rows(b, q, first):
                act.wait_ge(centred_set, b + 1)
                act.wait_ge(rstd_set, b + 1)
                if not first:
                    act.wait_ge(result_set, b - 1)
                nc.scalar.activation(scaled[:, q, :], centred[:, q, :], ACT.Copy, scale=rstd[:, q:q + 1]).then_inc(scaled_set, 1)

            def store(b, q):
                act.wait_ge(result_set, b + 1)
                act.dma_start(out[b, :, :], result[:, q, :]).then_inc(out_stored[q], 16)

            exponentials(0, 0, True)
            exponentials(1, 1, True)
            act.wait_ge(rows_in, 48)
            for b in (2, 3):
                q = b % 2
                upper_U(b - 2, q, True)
                value_bias(b - 2, q, True)
                if b == 3:
                    store(0, 0)
                exponentials(b, q, False)
                scale_rows(b - 2, q, True)
            with act.Fori(4, B - 1, 2) as b0:
                for q in range(2):
                    b = b0 + q
                    upper_U(b - 2, q, False)
                    value_bias(b - 2, q, False)
                    store(b - 3, 1 - q)
                    exponentials(b, q, False)
                    scale_rows(b - 2, q, False)
            for b in (B, B + 1):
                q = b % 2
                upper_U(b - 2, q, False)
                value_bias(b - 2, q, False)
                store(b - 3, 1 - q)
                scale_rows(b - 2, q, False)
            store(B - 1, 1)
            act.wait_ge(out_stored[0], 8 * B)
            act.wait_ge(out_stored[1], 8 * B)

        @block.vector
        def _(dve):
            nc.vector.memset(ones[:, :], 1.0).then_inc(consts_set, 1)
            nc.vector.memset(neg_half[:, :], -0.5).then_inc(consts_set, 1)
            nc.vector.memset(ps_scores(MC - 1), 0.0).then_inc(scores_zeroed, 1)
            dve.wait_ge(small_in, 32)
            nc.vector.tensor_copy(wkT[:, :, L:L + 1], bk_in[:, :].unsqueeze(2)).then_inc(bkcol_set, 1)
            nc.vector.tensor_copy(bk_wide[:, :, :], bk_in[:, :].unsqueeze(2).to_broadcast([P, EC, P])).then_inc(bkcol_set, 1)

            banks = [ps_U[:, 0, :], ps_U[:, 1, :], ps_Y[:, 0, :], ps_Y[:, 1, :]]
            dve.wait_ge(W_summed, 1)
            for e in range(EC):
                dve.wait_ge(Whi_set, e + 1)
                nc.vector.tensor_scalar(u_col[:, e:e + 1], banks[e][:, L:L + 1], SCALE, None, ALU.mult).then_inc(u_set, 1)
                nc.vector.scalar_tensor_tensor(W_lo[:, e, :], banks[e][:, 0:L], SCALE, W_hi[:, e, :].bitcast(F32),
                                               ALU.mult, ALU.subtract).then_inc(Wlo_set, 1)
            dve.wait_ge(u_set, EC)
            for g in range(NG):
                q = g % 2
                dve.wait_ge(xThi_set, g + 1)
                if g >= 2:
                    dve.wait_ge(G_summed, g - 1)
                nc.vector.tensor_tensor(xT_lo[:, q, :, :], xT_in[:, q, :, :], xT_hi[:, q, :, :].bitcast(F32),
                                        ALU.subtract).then_inc(xTlo_set, 1)
                if g >= 2:
                    dve.wait_ge(c_summed, g - 1)
                nc.vector.tensor_scalar(xu[:, q, 0, :], xT_in[:, q, 0, :], u_col[:, 0:1], None,
                                        ALU.mult).then_inc(xu_step, 1)
                for e in range(1, EC):
                    dve.wait_ge(xu_step, EC * g + e)
                    nc.vector.scalar_tensor_tensor(xu[:, q, e, :], xT_in[:, q, e, :], u_col[:, e:e + 1],
                                                   xu[:, q, e - 1, :], ALU.mult, ALU.add).then_inc(xu_step, 1)
            dve.wait_ge(Wvhi_set, 1)
            nc.vector.tensor_tensor(Wv_lo[:, :, :], wv_in[:, :, :], Wv_hi[:, :, :].bitcast(F32),
                                    ALU.subtract).then_inc(Wvlo_set, 1)
            dve.wait_ge(c_set, NG)
            dve.wait_ge(mask_set, 2)

            def maxima(b, q, first):
                dve.wait_ge(S_done, b + 1)
                if not first:
                    dve.wait_ge(exp_done, b - 1)
                shift = c_rows[0:MP, bass.ds(b * T, T)].unsqueeze(1).unsqueeze(1).to_broadcast([MP, 2, HALF, T])
                nc.vector.tensor_tensor(split_chunks(scores[0:MP, q, :]),
                                        ps_S[0:MP, :, 0:HALF * T].rearrange("p b (c t) -> p b c t", t=T),
                                        shift, ALU.add).then_inc(S_read, 1)
                dve.wait_ge(S_read, b + 1)
                nc.vector.tensor_reduce(negmax[0:MP, q, :], scores[0:MP, q, :].rearrange("p (c t) -> p c t", t=T),
                                        AX.X, ALU.max, negate=True).then_inc(negmax_set, 1)

            def normaliser(b, q):
                dve.wait_ge(exp_done, b + 1)
                nc.vector.reciprocal(rall[0:MP, q, :], expsum[0:MP, q, :]).then_inc(rall_set, 1)
                dve.wait_ge(rall_set, b + 1)
                nc.vector.tensor_tensor(rinv[0:MP, q, :], rall[0:MP, q, :], mask[0:MP, :], ALU.mult).then_inc(rinv_set, 1)

            def chunk_sum(b, q, first):
                dve.wait_ge(prob_set, b + 1)
                if not first:
                    dve.wait_ge(wsum_done, b - 1)
                nc.vector.tensor_reduce(probsum[0:MP, q, :], prob[0:MP, q, :].rearrange("p (c t) -> p t c", t=T),
                                        AX.X, ALU.add).then_inc(probsum_set, 1)

            def lower_U(b, q):
                dve.wait_ge(Uhi_set, b + 1)
                nc.vector.tensor_tensor(U_lo[:, q, :], ps_U[:, q, 0:LC * T], U_hi[:, q, :].bitcast(F32),
                                        ALU.subtract).then_inc(Ulo_set, 1)

            def row_stats(b, q):
                dve.wait_ge(Y_done, b + 1)
                dve.wait_ge(resid_set, b + 1)
                nc.vector.tensor_tensor(y[:, q, :], ps_Y[0:T, q, :], resid[:, q, :], ALU.add).then_inc(y_set, 1)
                dve.wait_ge(y_set, b + 1)
                nc.vector.bn_stats(stats[:, q, :], y[:, q, :]).then_inc(stats_set, 1)
                dve.wait_ge(stats_set, b + 1)

            def centre(b, q, first):
                nc.vector.bn_aggr(meanvar[:, q, :], stats[:, q, :]).then_inc(meanvar_set, 1)
                dve.wait_ge(meanvar_set, b + 1)
                if not first:
                    dve.wait_ge(scaled_set, b - 1)
                nc.vector.tensor_scalar(vareps[:, q:q + 1], meanvar[:, q, 1:2], EPS, None, ALU.add).then_inc(vareps_set, 1)
                nc.vector.scalar_tensor_tensor(centred[:, q, :], y[:, q, :], meanvar[:, q, 0:1], gamma_rows[:, :],
                                               ALU.subtract, ALU.mult).then_inc(centred_set, 1)

            dve.wait_ge(scores_zeroed, 1)
            maxima(0, 0, True)
            normaliser(0, 0)
            maxima(1, 1, True)
            chunk_sum(0, 0, True)
            dve.wait_ge(rows_in, 48)
            for b in (2, 3):
                q = b % 2
                normaliser(b - 1, 1 - q)
                lower_U(b - 2, q)
                maxima(b, q, False)
                row_stats(b - 2, q)
                chunk_sum(b - 1, 1 - q, b == 2)
                centre(b - 2, q, True)
            with dve.Fori(4, B - 1, 2) as b0:
                for q in range(2):
                    b = b0 + q
                    normaliser(b - 1, 1 - q)
                    lower_U(b - 2, q)
                    maxima(b, q, False)
                    row_stats(b - 2, q)
                    chunk_sum(b - 1, 1 - q, False)
                    centre(b - 2, q, False)
            normaliser(B - 1, 1)
            lower_U(B - 2, 0)
            chunk_sum(B - 1, 1, False)
            row_stats(B - 2, 0)
            centre(B - 2, 0, False)
            lower_U(B - 1, 1)
            row_stats(B - 1, 1)
            centre(B - 1, 1, False)

        @block.gpsimd
        def _(pool):
            nc.gpsimd.memset(mask[:, :], 1.0).then_inc(mask_set, 1)
            pool.wait_ge(mask_set, 1)
            nc.gpsimd.affine_select(out=mask[:, MC - 1:MC], in_=mask[:, MC - 1:MC], compare_op=ALU.is_ge, fill=0.0,
                                    base=ML - 1, pattern=[[0, 1]], channel_multiplier=-1).then_inc(mask_set, 1)

            def probabilities(b, q, first):
                pool.wait_ge(rinv_set, b + 1)
                if not first:
                    pool.wait_ge(U_done, b - 1)
                    pool.wait_ge(probsum_set, b - 1)
                nc.gpsimd.tensor_tensor(prob[0:MP, q, :].rearrange("p (c t) -> p c t", t=T),
                                        expo[0:MP, q, :].rearrange("p (c t) -> p c t", t=T),
                                        rinv[0:MP, q, :].unsqueeze(2).to_broadcast([MP, MC, T]),
                                        ALU.mult).then_inc(prob_set, 1)

            def residual(b, q, first):
                pool.wait_ge(x_loaded[q], 8 * (b - q) + 16)
                pool.wait_ge(bvw_set, b + 1)
                if not first:
                    pool.wait_ge(y_set, b - 1)
                nc.gpsimd.tensor_tensor(resid[:, q, :], x_in[:, q, :], bvw[:, q, :], ALU.add).then_inc(resid_set, 1)

            def inverse_deviation(b, q):
                pool.wait_ge(vareps_set, b + 1)
                nc.gpsimd.tensor_tensor(rstd[:, q:q + 1], vareps[:, q:q + 1], neg_half[:, :], ALU.pow).then_inc(rstd_set, 1)

            def finish(b, q, first):
                pool.wait_ge(scaled_set, b + 1)
                if not first:
                    pool.wait_ge(out_stored[q], 8 * (b - q))
                nc.gpsimd.tensor_tensor(result[:, q, :], scaled[:, q, :], beta_rows[:, :], ALU.add).then_inc(result_set, 1)

            pool.wait_ge(mask_set, 2)
            pool.wait_ge(consts_set, 2)
            probabilities(0, 0, True)
            pool.wait_ge(rows_in, 48)
            for b in (2, 3):
                q = b % 2
                probabilities(b - 1, 1 - q, b == 2)
                residual(b - 2, q, True)
                inverse_deviation(b - 2, q)
                finish(b - 2, q, True)
            with pool.Fori(4, B - 1, 2) as b0:
                for q in range(2):
                    b = b0 + q
                    probabilities(b - 1, 1 - q, False)
                    residual(b - 2, q, False)
                    inverse_deviation(b - 2, q)
                    finish(b - 2, q, False)
            probabilities(B - 1, 1, False)
            for b in (B - 2, B - 1):
                residual(b, b % 2, False)
                inverse_deviation(b, b % 2)
                finish(b, b % 2, False)


def kernel(x, ctx_512, L0_xattn_Wq, L0_xattn_bq, L0_xattn_Wk, L0_xattn_bk, L0_xattn_Wv, L0_xattn_bv,
           L0_xattn_gamma, L0_xattn_beta):
    import numpy as np
    import concourse.bacc as bacc
    from concourse.bass_utils import run_bass_kernel_spmd

    x = np.asarray(x)
    ctx = np.asarray(ctx_512)
    B, T, E = x.shape
    groups = 4
    arrays = {
        "xT": np.ascontiguousarray(x.reshape(groups, B // groups * T, E).transpose(0, 2, 1)),
        "x": np.ascontiguousarray(x),
        "ctxT": np.ascontiguousarray(ctx.transpose(0, 2, 1)),
        "ctx": np.ascontiguousarray(ctx),
        "WqT": np.ascontiguousarray(np.asarray(L0_xattn_Wq).T),
        "WkT": np.ascontiguousarray(np.asarray(L0_xattn_Wk).T),
        "bq": np.asarray(L0_xattn_bq),
        "bk": np.asarray(L0_xattn_bk),
        "Wv": np.asarray(L0_xattn_Wv),
        "bv": np.asarray(L0_xattn_bv),
        "gamma": np.asarray(L0_xattn_gamma),
        "beta": np.asarray(L0_xattn_beta),
    }
    nc = bacc.Bacc("TRN2", target_bir_lowering=False, num_devices=1)
    args = [nc.dram_tensor(n, a.shape, F32, kind="ExternalInput").ap() for n, a in arrays.items()]
    out = nc.dram_tensor("out", x.shape, F32, kind="ExternalOutput").ap()
    xattn(nc, *args, out)
    return run_bass_kernel_spmd(nc, [arrays], core_ids=[0]).results[0]["out"]
```

```python
from contextlib import ExitStack

import concourse.bass as bass
from concourse import mybir

ALU = mybir.AluOpType
ACT = mybir.ActivationFunctionType
AX = mybir.AxisListType
F32 = mybir.dt.float32
F32R = mybir.dt.float32r

P = 128
EPS = 1e-6


def xattn(nc, xT, x, ctxT, ctx, WqT, WkT, bq, bk, Wv, bv, gamma, beta, out):
    B, T, E = x.shape
    _, M, L = ctx.shape
    EC, LC = E // P, L // P
    MC = 6
    MP = -(-M // MC)
    ML = M - (MC - 1) * MP
    HALF = MC // 2
    GB = 4
    NG = B // GB
    GT = GB * T
    SCALE = float(E) ** -0.5
    assert HALF * T <= 512 and GT <= 512 and NG % 2 == 0 and B % 2 == 0

    with ExitStack() as stack:
        def sb(name, shape, dt=F32):
            return stack.enter_context(nc.sbuf_tensor(name, shape, dt))

        def ps(name, shape):
            return stack.enter_context(nc.psum_tensor(name, shape, F32))

        def sem(name):
            return stack.enter_context(nc.semaphore(name))

        wqT = sb("wqT", [P, EC, E])
        wkT = sb("wkT", [P, EC, L + 1])
        bk_in = sb("bk_in", [P, EC])
        bk_wide = sb("bk_wide", [P, EC, P])
        bq_col = sb("bq_col", [P, EC])
        W_hi = sb("W_hi", [P, EC, L], F32R)
        W_lo = sb("W_lo", [P, EC, L], F32R)
        u_col = sb("u_col", [P, EC])
        g_bias = sb("g_bias", [P, LC])
        c_bias = sb("c_bias", [P, 1])
        wv_in = sb("wv_in", [P, LC, E])
        Wv_hi = sb("Wv_hi", [P, LC, E], F32R)
        Wv_lo = sb("Wv_lo", [P, LC, E], F32R)
        bv_rows = sb("bv_rows", [T, E])
        gamma_rows = sb("gamma_rows", [T, E])
        beta_rows = sb("beta_rows", [T, E])
        ones = sb("ones", [P, P])
        mask = sb("mask", [P, MC])
        neg_half = sb("neg_half", [T, 1])
        xT_in = sb("xT_in", [P, 2, EC, GT])
        xT_hi = sb("xT_hi", [P, 2, EC, GT], F32R)
        xT_lo = sb("xT_lo", [P, 2, EC, GT], F32R)
        xu = sb("xu", [P, 2, EC, GT])
        G = sb("G", [P, LC, B * T])
        c_rows = sb("c_rows", [P, B * T])
        ctxT_in = sb("ctxT_in", [P, 2, LC, M])
        ctx_in = sb("ctx_in", [P, 2, MC, L])
        x_in = sb("x_in", [T, 2, E])
        scores = sb("scores", [P, 2, MC * T])
        negmax = sb("negmax", [P, 2, MC])
        expo = sb("expo", [P, 2, MC * T])
        expsum = sb("expsum", [P, 2, MC])
        rall = sb("rall", [P, 2, MC])
        rinv = sb("rinv", [P, 2, MC])
        prob = sb("prob", [P, 2, MC * T])
        probsum = sb("probsum", [P, 2, T])
        U_hi = sb("U_hi", [P, 2, LC * T], F32R)
        U_lo = sb("U_lo", [P, 2, LC * T], F32R)
        wsum = sb("wsum", [T, 2])
        bvw = sb("bvw", [T, 2, E])
        resid = sb("resid", [T, 2, E])
        y = sb("y", [T, 2, E])
        stats = sb("stats", [T, 2, 6])
        meanvar = sb("meanvar", [T, 2, 2])
        vareps = sb("vareps", [T, 2])
        rstd = sb("rstd", [T, 2])
        centred = sb("centred", [T, 2, E])
        scaled = sb("scaled", [T, 2, E])
        result = sb("result", [T, 2, E])

        ps_S = ps("ps_S", [P, 2, 512])
        ps_U = ps("ps_U", [P, 2, 512])
        ps_Y = ps("ps_Y", [P, 2, 512])
        ps_w = ps("ps_w", [P, 512])
        ps_c = ps("ps_c", [P, 512])

        wk_in = sem("wk_in")
        wq_in = [sem(f"wq_in{c}") for c in range(EC)]
        small_in = sem("small_in")
        xT_loaded = [sem(f"xT_loaded{q}") for q in range(2)]
        wv_loaded = sem("wv_loaded")
        rows_in = sem("rows_in")
        ctxT_loaded = [sem(f"ctxT_loaded{q}") for q in range(2)]
        ctx_loaded = [sem(f"ctx_loaded{q}") for q in range(2)]
        x_loaded = [sem(f"x_loaded{q}") for q in range(2)]
        out_stored = [sem(f"out_stored{q}") for q in range(2)]
        consts_set = sem("consts_set")
        bkcol_set = sem("bkcol_set")
        scores_zeroed = sem("scores_zeroed")
        W_summed = sem("W_summed")
        gbias_summed = sem("gbias_summed")
        cbias_summed = sem("cbias_summed")
        Whi_set = sem("Whi_set")
        Wlo_set = sem("Wlo_set")
        u_set = sem("u_set")
        gbias_set = sem("gbias_set")
        cbias_set = sem("cbias_set")
        Wvhi_set = sem("Wvhi_set")
        Wvlo_set = sem("Wvlo_set")
        mask_set = sem("mask_set")
        xThi_set = sem("xThi_set")
        xTlo_set = sem("xTlo_set")
        xu_step = sem("xu_step")
        G_summed = sem("G_summed")
        c_summed = sem("c_summed")
        G_set = sem("G_set")
        c_set = sem("c_set")
        S_done = sem("S_done")
        S_read = sem("S_read")
        negmax_set = sem("negmax_set")
        exp_done = sem("exp_done")
        rall_set = sem("rall_set")
        rinv_set = sem("rinv_set")
        prob_set = sem("prob_set")
        probsum_set = sem("probsum_set")
        U_done = sem("U_done")
        Uhi_set = sem("Uhi_set")
        Ulo_set = sem("Ulo_set")
        wsum_done = sem("wsum_done")
        wsum_set = sem("wsum_set")
        bvw_set = sem("bvw_set")
        resid_set = sem("resid_set")
        Y_done = sem("Y_done")
        y_set = sem("y_set")
        stats_set = sem("stats_set")
        meanvar_set = sem("meanvar_set")
        vareps_set = sem("vareps_set")
        rstd_set = sem("rstd_set")
        centred_set = sem("centred_set")
        scaled_set = sem("scaled_set")
        result_set = sem("result_set")

        def rows(c):
            return ML if c == MC - 1 else MP

        def ps_scores(c):
            return ps_S[:, c // HALF, (c % HALF) * T:(c % HALF + 1) * T]

        def split_chunks(ap):
            return ap.rearrange("p (b c t) -> p b c t", b=2, t=T)

        def loop(engine, start, stop, step):
            return nc.Fori(start, stop, step, engines=(engine.engine,), hint_back_edge=True)

        def first_two(b):
            return isinstance(b, int) and b < 2

        FIRST, AFTER = 6, B + 3

        def each_turn(engine, turn, first=0):
            for b in range(first, FIRST):
                turn(b, b % 2)
            with loop(engine, FIRST, B - 1, 2) as b0:
                for q in range(2):
                    turn(b0 + q, q)
            for b in range(B, AFTER + 1):
                turn(b, b % 2)

        def exists(b):
            return not isinstance(b, int) or 0 <= b < B

        block = stack.enter_context(nc.Block())

        @block.sync
        def _(sp):
            sp.dma_start(wkT[:, :, 0:L], WkT.rearrange("(p c) l -> p c l", c=EC)).then_inc(wk_in, 16)
            for c in range(EC):
                sp.dma_start(wqT[:, c, :], WqT.rearrange("(p c) e -> p c e", c=EC)[:, c, :]).then_inc(wq_in[c], 16)

            def load_group(g):
                if g >= 2:
                    sp.wait_ge(xThi_set, g - 1)
                    sp.wait_ge(xTlo_set, g - 1)
                    sp.wait_ge(xu_step, EC * (g - 1))
                sp.dma_start(xT_in[:, g % 2, :, :], xT[g].rearrange("(c p) t -> p c t", p=P)).then_inc(xT_loaded[g % 2], 16)

            def load_ctxT(b, q):
                sp.dma_start(ctxT_in[:, q, :, :], ctxT[b].rearrange("(c p) m -> p c m", p=P)).then_inc(ctxT_loaded[q], 16)

            def load_ctx(b, q):
                full = (MC - 1) * MP
                sp.dma_start(ctx_in[0:MP, q, 0:MC - 1, :],
                             ctx[b, 0:full, :].rearrange("(c p) l -> p c l", p=MP)).then_inc(ctx_loaded[q], 16)
                sp.dma_start(ctx_in[0:ML, q, MC - 1, :], ctx[b, full:M, :]).then_inc(ctx_loaded[q], 16)

            def load_x(b, q):
                sp.dma_start(x_in[:, q, :], x[b, :, :]).then_inc(x_loaded[q], 16)

            load_group(0)
            load_group(1)
            load_ctxT(0, 0)
            load_group(2)
            load_ctxT(1, 1)
            load_ctx(0, 0)
            load_group(3)
            sp.dma_start(wv_in[:, :, :], Wv.rearrange("(c p) e -> p c e", p=P)).then_inc(wv_loaded, 16)
            load_x(0, 0)
            load_ctx(1, 1)
            load_x(1, 1)

            def next_ctxT(b, q):
                sp.wait_ge(S_done, b - 1)
                load_ctxT(b, q)

            def next_ctx(b, q):
                sp.wait_ge(U_done, b - 1)
                load_ctx(b, q)

            def next_x(b, q):
                sp.wait_ge(resid_set, b - 1)
                load_x(b, q)

            next_ctxT(2, 0)
            next_ctxT(3, 1)
            next_ctxT(4, 0)
            next_ctx(2, 0)
            with loop(sp, 3, B - 4, 2) as b0:
                for n in range(2):
                    b, q = b0 + n, (n + 1) % 2
                    next_x(b - 1, 1 - q)
                    next_ctxT(b + 2, q)
                    next_ctx(b, q)
            for b in range(B - 3, B + 1):
                next_x(b - 1, (b - 1) % 2)
                if b + 2 < B:
                    next_ctxT(b + 2, b % 2)
                if b < B:
                    next_ctx(b, b % 2)

        @block.tensor
        def _(pe):
            banks = [ps_S[:, 0, :], ps_S[:, 1, :], ps_U[:, 0, :], ps_U[:, 1, :]]
            pe.wait_ge(wk_in, 16)
            pe.wait_ge(bkcol_set, 1)
            for f in range(EC):
                pe.wait_ge(wq_in[f], 16)
                for e in range(EC):
                    last = nc.tensor.matmul(banks[e][:, 0:L + 1], wqT[:, f, e * P:(e + 1) * P], wkT[:, f, :],
                                            start=(f == 0), stop=(f == EC - 1))
                    if f == EC - 1:
                        last.then_inc(W_summed, 1)
            pe.wait_ge(small_in, 32)
            for c in range(LC):
                for f in range(EC):
                    last = nc.tensor.matmul(ps_w[:, c:c + 1], wkT[:, f, c * P:(c + 1) * P], bq_col[:, f:f + 1],
                                            start=(f == 0), stop=(f == EC - 1))
            last.then_inc(gbias_summed, 1)
            pe.wait_ge(bkcol_set, 2)
            for f in range(EC):
                last = nc.tensor.matmul(ps_c[:, 0:1], bk_wide[:, f, :], bq_col[:, f:f + 1],
                                        start=(f == 0), stop=(f == EC - 1))
            last.then_inc(cbias_summed, 1)

            def project(g):
                q = g % 2
                bank = ps_Y if q == 0 else ps_U
                pe.wait_ge(xThi_set, g + 1)
                pe.wait_ge(xTlo_set, g + 1)
                if g == 1:
                    pe.wait_ge(Wlo_set, EC)
                if g >= 2:
                    pe.wait_ge(G_set, g - 1)
                n = 0
                for wpart, xpart in ((W_hi, xT_hi), (W_hi, xT_lo), (W_lo, xT_hi)):
                    for e in range(EC):
                        if g == 0 and xpart is xT_hi:
                            pe.wait_ge(Whi_set if wpart is W_hi else Wlo_set, e + 1)
                        for c in range(LC):
                            last = nc.tensor.matmul(bank[:, c, 0:GT], wpart[:, e, c * P:(c + 1) * P],
                                                    xpart[:, q, e, :], start=(n == 0), stop=(n == 3 * EC - 1))
                        n += 1
                last.then_inc(G_summed, 1)

            def sum_shift(g):
                pe.wait_ge(xu_step, EC * (g + 1))
                if g >= 1:
                    pe.wait_ge(c_set, g)
                else:
                    pe.wait_ge(cbias_set, 1)
                nc.tensor.matmul(ps_c[:, 0:GT], ones[:, :], xu[:, g % 2, EC - 1, :], start=True, stop=True).then_inc(c_summed, 1)

            def scores_of(b, q):
                pe.wait_ge(ctxT_loaded[q], 8 * (b - q) + 16)
                if isinstance(b, int):
                    pe.wait_ge(G_set, min(b // GB + 1, NG) if b < 2 else NG)
                if not (isinstance(b, int) and b == 0):
                    pe.wait_ge(S_read, b)
                else:
                    pe.wait_ge(scores_zeroed, 1)
                for c in range(MC):
                    for l in range(LC):
                        last = nc.tensor.matmul(ps_scores(c)[0:rows(c), :],
                                                ctxT_in[:, q, l, c * MP:c * MP + rows(c)],
                                                G[:, l, bass.ds(b * T, T)], start=(l == 0), stop=(l == LC - 1))
                last.then_inc(S_done, 1)

            def weighted_ctx(b, q):
                pe.wait_ge(ctx_loaded[q], 16 * (b - q) + 32)
                pe.wait_ge(prob_set, b + 1)
                if not first_two(b):
                    pe.wait_ge(Ulo_set, b - 1)
                for l in range(LC):
                    for c in range(MC):
                        last = nc.tensor.matmul(ps_U[:, q, l * T:(l + 1) * T],
                                                ctx_in[0:rows(c), q, c, l * P:(l + 1) * P],
                                                prob[0:rows(c), q, c * T:(c + 1) * T], start=(c == 0), stop=(c == MC - 1))
                last.then_inc(U_done, 1)

            def weight_sum(b, q):
                pe.wait_ge(probsum_set, b + 1)
                if not (isinstance(b, int) and b == 0):
                    pe.wait_ge(wsum_set, b)
                nc.tensor.matmul(ps_w[0:T, 0:1], probsum[0:MP, q, :], ones[0:MP, 0:1], start=True, stop=True).then_inc(wsum_done, 1)

            def values(b, q):
                pe.wait_ge(Uhi_set, b + 1)
                pe.wait_ge(Ulo_set, b + 1)
                if not first_two(b):
                    pe.wait_ge(y_set, b - 1)
                n = 0
                for upart, vpart in ((U_hi, Wv_hi), (U_hi, Wv_lo), (U_lo, Wv_hi)):
                    for l in range(LC):
                        last = nc.tensor.matmul(ps_Y[0:T, q, :], upart[:, q, l * T:(l + 1) * T], vpart[:, l, :],
                                                start=(n == 0), stop=(n == 3 * LC - 1))
                        n += 1
                last.then_inc(Y_done, 1)

            def turn(b, q):
                if exists(b):
                    scores_of(b, q)
                if exists(b - 3):
                    values(b - 3, 1 - q)
                if exists(b - 2):
                    weighted_ctx(b - 2, q)
                    weight_sum(b - 2, q)

            project(0)
            project(1)
            sum_shift(0)
            scores_of(0, 0)
            sum_shift(1)
            project(2)
            sum_shift(2)
            scores_of(1, 1)
            project(3)
            sum_shift(3)
            pe.wait_ge(Wvhi_set, 1)
            pe.wait_ge(Wvlo_set, 1)
            each_turn(pe, turn, 2)

        @block.scalar
        def _(act):
            with nc.allow_non_contiguous_dma("small constants"):
                act.dma_start(bk_in[:, :], bk.rearrange("(p c) -> p c", c=EC)).then_inc(small_in, 16)
                act.dma_start(bq_col[:, :], bq.rearrange("(p c) -> p c", c=EC)).then_inc(small_in, 16)
            act.dma_start(bv_rows[:, :], bv.partition_broadcast(T)).then_inc(rows_in, 16)
            act.dma_start(gamma_rows[:, :], gamma.partition_broadcast(T)).then_inc(rows_in, 16)
            act.dma_start(beta_rows[:, :], beta.partition_broadcast(T)).then_inc(rows_in, 16)

            def upper_half(g):
                q = g % 2
                act.wait_ge(xT_loaded[q], 8 * (g - q) + 16)
                if g >= 2:
                    act.wait_ge(G_summed, g - 1)
                nc.scalar.activation(xT_hi[:, q, :, :], xT_in[:, q, :, :], ACT.Copy).then_inc(xThi_set, 1)

            def take_group(g):
                bank = ps_Y if g % 2 == 0 else ps_U
                act.wait_ge(G_summed, g + 1)
                for c in range(LC):
                    last = nc.scalar.activation(G[:, c, g * GT:(g + 1) * GT], bank[:, c, 0:GT], ACT.Identity,
                                                bias=g_bias[:, c:c + 1])
                last.then_inc(G_set, 1)

            def take_shift(g):
                act.wait_ge(c_summed, g + 1)
                nc.scalar.activation(c_rows[:, g * GT:(g + 1) * GT], ps_c[:, 0:GT], ACT.Identity,
                                     bias=c_bias[:, 0:1]).then_inc(c_set, 1)

            def exponentials(b, q):
                act.wait_ge(negmax_set, b + 1)
                if not first_two(b):
                    act.wait_ge(prob_set, b - 1)
                for c in range(MC):
                    last = nc.scalar.activation(expo[0:MP, q, c * T:(c + 1) * T], scores[0:MP, q, c * T:(c + 1) * T],
                                                ACT.Exp, bias=negmax[0:MP, q, c:c + 1],
                                                accum_out=expsum[0:MP, q, c:c + 1])
                last.then_inc(exp_done, 1)

            def upper_U(b, q):
                act.wait_ge(U_done, b + 1)
                if not first_two(b):
                    act.wait_ge(Y_done, b - 1)
                nc.scalar.activation(U_hi[:, q, :], ps_U[:, q, 0:LC * T], ACT.Copy).then_inc(Uhi_set, 1)

            def value_bias(b, q):
                act.wait_ge(wsum_done, b + 1)
                nc.scalar.activation(wsum[:, q:q + 1], ps_w[0:T, 0:1], ACT.Copy).then_inc(wsum_set, 1)
                act.wait_ge(wsum_set, b + 1)
                if not first_two(b):
                    act.wait_ge(resid_set, b - 1)
                nc.scalar.activation(bvw[:, q, :], bv_rows[:, :], ACT.Copy, scale=wsum[:, q:q + 1]).then_inc(bvw_set, 1)

            def scale_rows(b, q):
                act.wait_ge(centred_set, b + 1)
                act.wait_ge(rstd_set, b + 1)
                if not first_two(b):
                    act.wait_ge(result_set, b - 1)
                nc.scalar.activation(scaled[:, q, :], centred[:, q, :], ACT.Copy, scale=rstd[:, q:q + 1]).then_inc(scaled_set, 1)

            def store(b, q):
                act.wait_ge(result_set, b + 1)
                act.dma_start(out[b, :, :], result[:, q, :]).then_inc(out_stored[q], 16)

            def turn(b, q):
                if exists(b - 3):
                    upper_U(b - 3, 1 - q)
                    value_bias(b - 3, 1 - q)
                if exists(b - 4):
                    store(b - 4, q)
                if exists(b):
                    exponentials(b, q)
                if exists(b - 3):
                    scale_rows(b - 3, 1 - q)

            banks = [ps_S[:, 0, :], ps_S[:, 1, :], ps_U[:, 0, :], ps_U[:, 1, :]]
            upper_half(0)
            upper_half(1)
            for e in range(EC):
                act.wait_ge(W_summed, e + 1)
                nc.scalar.activation(W_hi[:, e, :], banks[e][:, 0:L], ACT.Copy, scale=SCALE).then_inc(Whi_set, 1)
            act.wait_ge(gbias_summed, 1)
            nc.scalar.activation(g_bias[:, :], ps_w[:, 0:LC], ACT.Copy, scale=SCALE).then_inc(gbias_set, 1)
            act.wait_ge(cbias_summed, 1)
            nc.scalar.activation(c_bias[:, :], ps_c[:, 0:1], ACT.Copy, scale=SCALE).then_inc(cbias_set, 1)
            act.wait_ge(gbias_set, 1)
            act.wait_ge(cbias_set, 1)
            take_group(0)
            upper_half(2)
            take_group(1)
            take_shift(0)
            upper_half(3)
            exponentials(0, 0)
            take_shift(1)
            act.wait_ge(wv_loaded, 16)
            nc.scalar.activation(Wv_hi[:, :, :], wv_in[:, :, :], ACT.Copy).then_inc(Wvhi_set, 1)
            take_group(2)
            take_shift(2)
            exponentials(1, 1)
            take_group(3)
            take_shift(3)
            act.wait_ge(rows_in, 48)
            each_turn(act, turn, 2)
            act.wait_ge(out_stored[0], 8 * B)
            act.wait_ge(out_stored[1], 8 * B)

        @block.vector
        def _(dve):
            nc.vector.memset(ones[:, :], 1.0).then_inc(consts_set, 1)
            nc.vector.memset(neg_half[:, :], -0.5).then_inc(consts_set, 1)
            dve.wait_ge(small_in, 32)
            nc.vector.tensor_copy(wkT[:, :, L:L + 1], bk_in[:, :].unsqueeze(2)).then_inc(bkcol_set, 1)
            nc.vector.tensor_copy(bk_wide[:, :, :], bk_in[:, :].unsqueeze(2).to_broadcast([P, EC, P])).then_inc(bkcol_set, 1)

            banks = [ps_S[:, 0, :], ps_S[:, 1, :], ps_U[:, 0, :], ps_U[:, 1, :]]
            def lower_half(g):
                q = g % 2
                dve.wait_ge(xThi_set, g + 1)
                if g >= 2:
                    dve.wait_ge(G_summed, g - 1)
                nc.vector.tensor_tensor(xT_lo[:, q, :, :], xT_in[:, q, :, :], xT_hi[:, q, :, :].bitcast(F32),
                                        ALU.subtract).then_inc(xTlo_set, 1)

            def weigh_by_u(g):
                q = g % 2
                if g >= 2:
                    dve.wait_ge(c_summed, g - 1)
                nc.vector.tensor_scalar(xu[:, q, 0, :], xT_in[:, q, 0, :], u_col[:, 0:1], None,
                                        ALU.mult).then_inc(xu_step, 1)
                for e in range(1, EC):
                    dve.wait_ge(xu_step, EC * g + e)
                    nc.vector.scalar_tensor_tensor(xu[:, q, e, :], xT_in[:, q, e, :], u_col[:, e:e + 1],
                                                   xu[:, q, e - 1, :], ALU.mult, ALU.add).then_inc(xu_step, 1)

            def maxima(b, q):
                if isinstance(b, int) and b < B:
                    dve.wait_ge(c_set, b // GB + 1 if b < 2 else NG)
                dve.wait_ge(S_done, b + 1)
                if not first_two(b):
                    dve.wait_ge(exp_done, b - 1)
                shift = c_rows[0:MP, bass.ds(b * T, T)].unsqueeze(1).unsqueeze(1).to_broadcast([MP, 2, HALF, T])
                nc.vector.tensor_tensor(split_chunks(scores[0:MP, q, :]),
                                        ps_S[0:MP, :, 0:HALF * T].rearrange("p b (c t) -> p b c t", t=T),
                                        shift, ALU.add).then_inc(S_read, 1)
                dve.wait_ge(S_read, b + 1)
                nc.vector.tensor_reduce(negmax[0:MP, q, :], scores[0:MP, q, :].rearrange("p (c t) -> p c t", t=T),
                                        AX.X, ALU.max, negate=True).then_inc(negmax_set, 1)

            def normaliser(b, q):
                dve.wait_ge(exp_done, b + 1)
                nc.vector.reciprocal(rall[0:MP, q, :], expsum[0:MP, q, :]).then_inc(rall_set, 1)
                dve.wait_ge(rall_set, b + 1)
                nc.vector.tensor_tensor(rinv[0:MP, q, :], rall[0:MP, q, :], mask[0:MP, :], ALU.mult).then_inc(rinv_set, 1)

            def chunk_sum(b, q):
                dve.wait_ge(prob_set, b + 1)
                if not first_two(b):
                    dve.wait_ge(wsum_done, b - 1)
                nc.vector.tensor_reduce(probsum[0:MP, q, :], prob[0:MP, q, :].rearrange("p (c t) -> p t c", t=T),
                                        AX.X, ALU.add).then_inc(probsum_set, 1)

            def lower_U(b, q):
                dve.wait_ge(Uhi_set, b + 1)
                nc.vector.tensor_tensor(U_lo[:, q, :], ps_U[:, q, 0:LC * T], U_hi[:, q, :].bitcast(F32),
                                        ALU.subtract).then_inc(Ulo_set, 1)

            def row_stats(b, q):
                dve.wait_ge(Y_done, b + 1)
                dve.wait_ge(resid_set, b + 1)
                nc.vector.tensor_tensor(y[:, q, :], ps_Y[0:T, q, :], resid[:, q, :], ALU.add).then_inc(y_set, 1)
                dve.wait_ge(y_set, b + 1)
                nc.vector.bn_stats(stats[:, q, :], y[:, q, :]).then_inc(stats_set, 1)
                dve.wait_ge(stats_set, b + 1)

            def centre(b, q):
                nc.vector.bn_aggr(meanvar[:, q, :], stats[:, q, :]).then_inc(meanvar_set, 1)
                dve.wait_ge(meanvar_set, b + 1)
                if not first_two(b):
                    dve.wait_ge(scaled_set, b - 1)
                nc.vector.tensor_scalar(vareps[:, q:q + 1], meanvar[:, q, 1:2], EPS, None, ALU.add).then_inc(vareps_set, 1)
                nc.vector.scalar_tensor_tensor(centred[:, q, :], y[:, q, :], meanvar[:, q, 0:1], gamma_rows[:, :],
                                               ALU.subtract, ALU.mult).then_inc(centred_set, 1)

            def turn(b, q):
                if exists(b - 1):
                    normaliser(b - 1, 1 - q)
                if exists(b - 3):
                    lower_U(b - 3, 1 - q)
                if exists(b):
                    maxima(b, q)
                if exists(b - 3):
                    row_stats(b - 3, 1 - q)
                if exists(b - 1):
                    chunk_sum(b - 1, 1 - q)
                if exists(b - 3):
                    centre(b - 3, 1 - q)

            lower_half(0)
            lower_half(1)
            for e in range(EC):
                dve.wait_ge(Whi_set, e + 1)
                nc.vector.tensor_scalar(u_col[:, e:e + 1], banks[e][:, L:L + 1], SCALE, None, ALU.mult).then_inc(u_set, 1)
                nc.vector.scalar_tensor_tensor(W_lo[:, e, :], banks[e][:, 0:L], SCALE, W_hi[:, e, :].bitcast(F32),
                                               ALU.mult, ALU.subtract).then_inc(Wlo_set, 1)
            dve.wait_ge(Wlo_set, EC)
            nc.vector.memset(ps_scores(MC - 1), 0.0).then_inc(scores_zeroed, 1)
            dve.wait_ge(u_set, EC)
            weigh_by_u(0)
            weigh_by_u(1)
            lower_half(2)
            weigh_by_u(2)
            dve.wait_ge(mask_set, 2)
            dve.wait_ge(scores_zeroed, 1)
            maxima(0, 0)
            lower_half(3)
            weigh_by_u(3)
            dve.wait_ge(Wvhi_set, 1)
            nc.vector.tensor_tensor(Wv_lo[:, :, :], wv_in[:, :, :], Wv_hi[:, :, :].bitcast(F32),
                                    ALU.subtract).then_inc(Wvlo_set, 1)
            maxima(1, 1)
            normaliser(0, 0)
            chunk_sum(0, 0)
            dve.wait_ge(rows_in, 48)
            each_turn(dve, turn, 2)

        @block.gpsimd
        def _(pool):
            nc.gpsimd.memset(mask[:, :], 1.0).then_inc(mask_set, 1)
            pool.wait_ge(mask_set, 1)
            nc.gpsimd.affine_select(out=mask[:, MC - 1:MC], in_=mask[:, MC - 1:MC], compare_op=ALU.is_ge, fill=0.0,
                                    base=ML - 1, pattern=[[0, 1]], channel_multiplier=-1).then_inc(mask_set, 1)

            def probabilities(b, q):
                pool.wait_ge(rinv_set, b + 1)
                if not first_two(b):
                    pool.wait_ge(U_done, b - 1)
                    pool.wait_ge(probsum_set, b - 1)
                nc.gpsimd.tensor_tensor(prob[0:MP, q, :].rearrange("p (c t) -> p c t", t=T),
                                        expo[0:MP, q, :].rearrange("p (c t) -> p c t", t=T),
                                        rinv[0:MP, q, :].unsqueeze(2).to_broadcast([MP, MC, T]),
                                        ALU.mult).then_inc(prob_set, 1)

            def residual(b, q):
                pool.wait_ge(x_loaded[q], 8 * (b - q) + 16)
                pool.wait_ge(bvw_set, b + 1)
                if not first_two(b):
                    pool.wait_ge(y_set, b - 1)
                nc.gpsimd.tensor_tensor(resid[:, q, :], x_in[:, q, :], bvw[:, q, :], ALU.add).then_inc(resid_set, 1)

            def inverse_deviation(b, q):
                pool.wait_ge(vareps_set, b + 1)
                nc.gpsimd.tensor_tensor(rstd[:, q:q + 1], vareps[:, q:q + 1], neg_half[:, :], ALU.pow).then_inc(rstd_set, 1)

            def finish(b, q):
                pool.wait_ge(scaled_set, b + 1)
                if not first_two(b):
                    pool.wait_ge(out_stored[q], 8 * (b - q))
                nc.gpsimd.tensor_tensor(result[:, q, :], scaled[:, q, :], beta_rows[:, :], ALU.add).then_inc(result_set, 1)

            pool.wait_ge(mask_set, 2)
            pool.wait_ge(consts_set, 2)
            pool.wait_ge(rows_in, 48)

            def turn(b, q):
                if exists(b - 3):
                    residual(b - 3, 1 - q)
                if exists(b - 1):
                    probabilities(b - 1, 1 - q)
                if exists(b - 3):
                    inverse_deviation(b - 3, 1 - q)
                    finish(b - 3, 1 - q)

            each_turn(pool, turn, 1)


def kernel(x, ctx_512, L0_xattn_Wq, L0_xattn_bq, L0_xattn_Wk, L0_xattn_bk, L0_xattn_Wv, L0_xattn_bv,
           L0_xattn_gamma, L0_xattn_beta):
    import numpy as np
    import concourse.bacc as bacc
    from concourse.bass_utils import run_bass_kernel_spmd

    x = np.asarray(x)
    ctx = np.asarray(ctx_512)
    B, T, E = x.shape
    groups = 4
    arrays = {
        "xT": np.ascontiguousarray(x.reshape(groups, B // groups * T, E).transpose(0, 2, 1)),
        "x": np.ascontiguousarray(x),
        "ctxT": np.ascontiguousarray(ctx.transpose(0, 2, 1)),
        "ctx": np.ascontiguousarray(ctx),
        "WqT": np.ascontiguousarray(np.asarray(L0_xattn_Wq).T),
        "WkT": np.ascontiguousarray(np.asarray(L0_xattn_Wk).T),
        "bq": np.asarray(L0_xattn_bq),
        "bk": np.asarray(L0_xattn_bk),
        "Wv": np.asarray(L0_xattn_Wv),
        "bv": np.asarray(L0_xattn_bv),
        "gamma": np.asarray(L0_xattn_gamma),
        "beta": np.asarray(L0_xattn_beta),
    }
    nc = bacc.Bacc("TRN2", target_bir_lowering=False, num_devices=1)
    args = [nc.dram_tensor(n, a.shape, F32, kind="ExternalInput").ap() for n, a in arrays.items()]
    out = nc.dram_tensor("out", x.shape, F32, kind="ExternalOutput").ap()
    xattn(nc, *args, out)
    return run_bass_kernel_spmd(nc, [arrays], core_ids=[0]).results[0]["out"]
```

```python
from contextlib import ExitStack

import concourse.bass as bass
from concourse import mybir

ALU = mybir.AluOpType
ACT = mybir.ActivationFunctionType
AX = mybir.AxisListType
F32 = mybir.dt.float32
F32R = mybir.dt.float32r

P = 128
EPS = 1e-6


def xattn(nc, xT, x, ctxT, ctx, WqT, WkT, bq, bk, Wv, bv, gamma, beta, out):
    B, T, E = x.shape
    _, M, L = ctx.shape
    EC, LC = E // P, L // P
    MC = 6
    MP = -(-M // MC)
    ML = M - (MC - 1) * MP
    HALF = MC // 2
    GB = 4
    NG = B // GB
    GT = GB * T
    NX = 3
    EH = EC // 2
    SCALE = float(E) ** -0.5
    assert NG == NX + 1
    assert HALF * T <= 512 and GT <= 512 and NG % 2 == 0 and B % 2 == 0

    with ExitStack() as stack:
        def sb(name, shape, dt=F32):
            return stack.enter_context(nc.sbuf_tensor(name, shape, dt))

        def ps(name, shape):
            return stack.enter_context(nc.psum_tensor(name, shape, F32))

        def sem(name):
            return stack.enter_context(nc.semaphore(name))

        WARM = 9

        wqT = sb("wqT", [P, EC, E])
        wkT = sb("wkT", [P, EC, L + 2])
        wq_hi = sb("wq_hi", [P, EC, E], F32R)
        wq_lo = sb("wq_lo", [P, EC, E], F32R)
        wk_hi = sb("wk_hi", [P, EC, L + 2], F32R)
        wk_lo = sb("wk_lo", [P, EC, L + 2], F32R)
        bk_in = sb("bk_in", [P, EC])
        wkq = sb("wkq", [P, 2, L + 2])
        bq_col = sb("bq_col", [P, EC])
        W_hi = sb("W_hi", [P, EC, L], F32R)
        W_lo = sb("W_lo", [P, EC, L], F32R)
        u_col = sb("u_col", [P, EC])
        g_bias = sb("g_bias", [P, LC])
        bb_col = sb("bb_col", [P, 1])
        wv_in = sb("wv_in", [P, LC, E])
        Wv_hi = sb("Wv_hi", [P, LC, E], F32R)
        Wv_lo = sb("Wv_lo", [P, LC, E], F32R)
        bv_rows = sb("bv_rows", [T, E])
        gamma_rows = sb("gamma_rows", [T, E])
        beta_rows = sb("beta_rows", [T, E])
        ones = sb("ones", [P, P])
        ones_r = sb("ones_r", [P, P], F32R)
        mask = sb("mask", [P, MC])
        neg_half = sb("neg_half", [T, 1])
        xT_in = sb("xT_in", [P, NX, EC, GT])
        xT_hi = sb("xT_hi", [P, 2, EC, GT], F32R)
        xT_lo = sb("xT_lo", [P, 2, EC, GT], F32R)
        xu = sb("xu", [P, 2, GT])
        xu_hi = sb("xu_hi", [P, 2, GT], F32R)
        xu_lo = sb("xu_lo", [P, 2, GT], F32R)
        G = sb("G", [P, LC, B * T])
        c_rows = sb("c_rows", [P, B * T])
        ctxT_in = sb("ctxT_in", [P, 2, LC, M])
        ctx_in = sb("ctx_in", [P, 2, MC, L])
        x_in = sb("x_in", [T, 2, E])
        scores = sb("scores", [P, 2, MC * T])
        negmax = sb("negmax", [P, 2, MC])
        expo = sb("expo", [P, 2, MC * T])
        expsum = sb("expsum", [P, 2, MC])
        rall = sb("rall", [P, 2, MC])
        rinv = sb("rinv", [P, 2, MC])
        prob = sb("prob", [P, 2, MC * T])
        probsum = sb("probsum", [P, 2, T])
        U_hi = sb("U_hi", [P, 2, LC * T], F32R)
        U_lo = sb("U_lo", [P, 2, LC * T], F32R)
        wsum = sb("wsum", [T, 2])
        bvw = sb("bvw", [T, 2, E])
        resid = sb("resid", [T, 2, E])
        y = sb("y", [T, 2, E])
        stats = sb("stats", [T, 2, 6])
        meanvar = sb("meanvar", [T, 2, 2])
        vareps = sb("vareps", [T, 2])
        rstd = sb("rstd", [T, 2])
        centred = sb("centred", [T, 2, E])
        scaled = sb("scaled", [T, 2, E])
        result = sb("result", [T, 2, E])

        ps_S = ps("ps_S", [P, 2, 512])
        ps_U = ps("ps_U", [P, 2, 512])
        ps_Y = ps("ps_Y", [P, 2, 512])
        ps_w = ps("ps_w", [P, 512])
        ps_c = ps("ps_c", [P, 512])

        w_in = [sem(f"w_in{c}") for c in range(EC)]
        bk_loaded = sem("bk_loaded")
        bq_loaded = sem("bq_loaded")
        xT_loaded = [[sem(f"xT_loaded{g}_{h}") for h in range(2)] for g in range(NG)]
        wv_loaded = sem("wv_loaded")
        rows_in = sem("rows_in")
        ctxT_loaded = [sem(f"ctxT_loaded{q}") for q in range(2)]
        ctx_loaded = [sem(f"ctx_loaded{q}") for q in range(2)]
        x_loaded = [sem(f"x_loaded{q}") for q in range(2)]
        out_stored = [sem(f"out_stored{q}") for q in range(2)]
        consts_set = sem("consts_set")
        onesr_set = sem("onesr_set")
        bkcol_set = sem("bkcol_set")
        wqhi_set = sem("wqhi_set")
        wkhi_set = sem("wkhi_set")
        wqlo_set = sem("wqlo_set")
        wklo_set = sem("wklo_set")
        scores_zeroed = sem("scores_zeroed")
        W_summed = sem("W_summed")
        wkq_step = sem("wkq_step")
        gbias_summed = sem("gbias_summed")
        Whi_set = sem("Whi_set")
        Wlo_set = sem("Wlo_set")
        u_set = sem("u_set")
        gbias_set = sem("gbias_set")
        bb_set = sem("bb_set")
        Wvhi_set = sem("Wvhi_set")
        Wvlo_set = sem("Wvlo_set")
        mask_set = sem("mask_set")
        xThi_set = sem("xThi_set")
        xTlo_set = sem("xTlo_set")
        xu_step = sem("xu_step")
        xuhi_set = sem("xuhi_set")
        xulo_set = sem("xulo_set")
        G_summed = sem("G_summed")
        c_summed = sem("c_summed")
        G_set = sem("G_set")
        c_set = sem("c_set")
        S_done = sem("S_done")
        S_read = sem("S_read")
        negmax_set = sem("negmax_set")
        exp_done = sem("exp_done")
        rall_set = sem("rall_set")
        rinv_set = sem("rinv_set")
        prob_set = sem("prob_set")
        probsum_set = sem("probsum_set")
        U_done = sem("U_done")
        Uhi_set = sem("Uhi_set")
        Ulo_set = sem("Ulo_set")
        last_U_done = sem("last_U_done")
        last_Uhi_set = sem("last_Uhi_set")
        last_Ulo_set = sem("last_Ulo_set")
        wsum_done = sem("wsum_done")
        wsum_set = sem("wsum_set")
        bvw_set = sem("bvw_set")
        resid_set = sem("resid_set")
        Y_done = sem("Y_done")
        y_set = sem("y_set")
        stats_set = sem("stats_set")
        meanvar_set = sem("meanvar_set")
        vareps_set = sem("vareps_set")
        rstd_set = sem("rstd_set")
        centred_set = sem("centred_set")
        scaled_set = sem("scaled_set")
        result_set = sem("result_set")

        def rows(c):
            return ML if c == MC - 1 else MP

        def ps_scores(c):
            return ps_S[:, c // HALF, (c % HALF) * T:(c % HALF + 1) * T]

        def split_chunks(ap):
            return ap.rearrange("p (b c t) -> p b c t", b=2, t=T)

        def loop(engine, start, stop, step):
            return nc.Fori(start, stop, step, engines=(engine.engine,), hint_back_edge=True)

        def first_two(b):
            return isinstance(b, int) and b < 2

        FIRST = 6

        def each_turn(engine, turn, first):
            for b in range(first, FIRST):
                turn(b, b % 2)
            with loop(engine, FIRST, B - 1, 2) as b0:
                for q in range(2):
                    turn(b0 + q, q)

        def exists(b):
            return not isinstance(b, int) or 0 <= b < B

        block = stack.enter_context(nc.Block())

        @block.sync
        def _(sp):
            for c in range(EC):
                sp.dma_start(wqT[:, c, :], WqT.rearrange("(p c) e -> p c e", c=EC)[:, c, :]).then_inc(w_in[c], 16)
                sp.dma_start(wkT[:, c, 0:L], WkT.rearrange("(p c) l -> p c l", c=EC)[:, c, :]).then_inc(w_in[c], 16)

            def load_group(g):
                for h in range(2):
                    sp.dma_start(xT_in[:, g % NX, h * EH:(h + 1) * EH, :],
                                 xT[g].rearrange("(c p) t -> p c t", p=P)[:, h * EH:(h + 1) * EH, :]).then_inc(xT_loaded[g][h], 16)

            def load_ctxT(b, q):
                sp.dma_start(ctxT_in[:, q, :, :], ctxT[b].rearrange("(c p) m -> p c m", p=P)).then_inc(ctxT_loaded[q], 16)

            def load_ctx(b, q):
                full = (MC - 1) * MP
                sp.dma_start(ctx_in[0:MP, q, 0:MC - 1, :],
                             ctx[b, 0:full, :].rearrange("(c p) l -> p c l", p=MP)).then_inc(ctx_loaded[q], 16)
                sp.dma_start(ctx_in[0:ML, q, MC - 1, :], ctx[b, full:M, :]).then_inc(ctx_loaded[q], 16)

            def load_x(b, q):
                sp.dma_start(x_in[:, q, :], x[b, :, :]).then_inc(x_loaded[q], 16)

            load_group(0)
            load_group(1)
            load_ctxT(0, 0)
            load_group(2)
            load_ctxT(1, 1)
            sp.wait_ge(xTlo_set, 2)
            sp.wait_ge(xu_step, EC)
            load_group(3)
            for there, array in ((bv_rows, bv), (gamma_rows, gamma), (beta_rows, beta)):
                sp.dma_start(there[:, :], array.partition_broadcast(T)).then_inc(rows_in, 16)
            load_ctx(0, 0)
            sp.dma_start(wv_in[:, :, :], Wv.rearrange("(c p) e -> p c e", p=P)).then_inc(wv_loaded, 16)
            load_x(0, 0)
            load_ctx(1, 1)
            load_x(1, 1)

            def next_ctxT(b, q):
                sp.wait_ge(S_done, b - 1)
                load_ctxT(b, q)

            def next_ctx(b, q):
                sp.wait_ge(U_done, b - 1)
                load_ctx(b, q)

            def next_x(b, q):
                sp.wait_ge(resid_set, b - 1)
                load_x(b, q)

            next_ctxT(2, 0)
            next_ctxT(3, 1)
            next_ctxT(4, 0)
            next_ctx(2, 0)
            with loop(sp, 3, B - 4, 2) as b0:
                for n in range(2):
                    b, q = b0 + n, (n + 1) % 2
                    next_x(b - 1, 1 - q)
                    next_ctxT(b + 2, q)
                    next_ctx(b, q)
            for b in range(B - 3, B + 1):
                next_x(b - 1, (b - 1) % 2)
                if b + 2 < B:
                    next_ctxT(b + 2, b % 2)
                if b < B:
                    next_ctx(b, b % 2)
            for b in range(B - 4, B):
                sp.wait_ge(result_set, b + 1)
                source = scaled if b == B - 1 else result
                sp.dma_start(out[b, :, :], source[:, b % 2, :]).then_inc(out_stored[b % 2], 16)
            sp.wait_ge(out_stored[0], 8 * B)
            sp.wait_ge(out_stored[1], 8 * B)

        @block.tensor
        def _(pe):
            banks = [ps_S[:, 0, :], ps_S[:, 1, :], ps_U[:, 0, :], ps_U[:, 1, :]]
            pe.wait_ge(consts_set, 1)
            for _ in range(WARM):
                nc.tensor.matmul(ps_Y[:, 0, 0:P], ones[:, :], ones[:, :], start=True, stop=True)
            for f in range(EC):
                pe.wait_ge(wqhi_set, f + 1)
                pe.wait_ge(wkhi_set, f + 1)
                for e in range(EC):
                    nc.tensor.matmul(banks[e][:, 0:L + 2], wq_hi[:, f, e * P:(e + 1) * P], wk_hi[:, f, :],
                                     start=(f == 0), stop=False)
                pe.wait_ge(wklo_set, f + 1)
                pe.wait_ge(wqlo_set, f + 1)
                for e in range(EC):
                    nc.tensor.matmul(banks[e][:, 0:L + 2], wq_hi[:, f, e * P:(e + 1) * P], wk_lo[:, f, :],
                                     start=False, stop=False)
                    last = nc.tensor.matmul(banks[e][:, 0:L + 2], wq_lo[:, f, e * P:(e + 1) * P], wk_hi[:, f, :],
                                            start=False, stop=(f == EC - 1))
                    if f == EC - 1:
                        last.then_inc(W_summed, 1)
            def project(g):
                q = g % 2
                bank = ps_Y if q == 0 else ps_U
                pe.wait_ge(xThi_set, 2 * (g + 1))
                if g == 1:
                    pe.wait_ge(u_set, EC)
                if g >= 2:
                    pe.wait_ge(G_set, g - 1)
                n = 0
                for wpart, xpart in ((W_hi, xT_hi), (W_hi, xT_lo), (W_lo, xT_hi)):
                    if xpart is xT_lo:
                        pe.wait_ge(xTlo_set, 2 * (g + 1))
                    for e in range(EC):
                        if g == 0 and xpart is xT_hi:
                            pe.wait_ge(Whi_set if wpart is W_hi else Wlo_set, e + 1)
                        for c in range(LC):
                            last = nc.tensor.matmul(bank[:, c, 0:GT], wpart[:, e, c * P:(c + 1) * P],
                                                    xpart[:, q, e, :], start=(n == 0), stop=(n == 3 * EC - 1))
                        n += 1
                last.then_inc(G_summed, 1)

            def sum_shift(g):
                pe.wait_ge(xuhi_set, g + 1)
                pe.wait_ge(xulo_set, g + 1)
                if g >= 1:
                    pe.wait_ge(c_set, g)
                else:
                    pe.wait_ge(onesr_set, 1)
                nc.tensor.matmul(ps_c[:, 0:GT], ones_r[:, :], xu_hi[:, g % 2, :], start=True, stop=False)
                nc.tensor.matmul(ps_c[:, 0:GT], ones_r[:, :], xu_lo[:, g % 2, :], start=False, stop=True).then_inc(c_summed, 1)

            def scores_of(b, q):
                pe.wait_ge(ctxT_loaded[q], 8 * (b - q) + 16)
                if isinstance(b, int):
                    pe.wait_ge(G_set, NG if b == FIRST - 1 else b // GB + 1)
                if not (isinstance(b, int) and b == 0):
                    pe.wait_ge(S_read, b)
                else:
                    pe.wait_ge(scores_zeroed, 1)
                for c in range(MC):
                    for l in range(LC):
                        last = nc.tensor.matmul(ps_scores(c)[0:rows(c), :],
                                                ctxT_in[:, q, l, c * MP:c * MP + rows(c)],
                                                G[:, l, bass.ds(b * T, T)], start=(l == 0), stop=(l == LC - 1))
                last.then_inc(S_done, 1)

            def weighted_ctx(b, q):
                pe.wait_ge(ctx_loaded[q], 16 * (b - q) + 32)
                pe.wait_ge(prob_set, b + 1)
                if not first_two(b):
                    pe.wait_ge(Ulo_set, b - 1)
                else:
                    pe.wait_ge(G_set, NG)
                for l in range(LC):
                    for c in range(MC):
                        last = nc.tensor.matmul(ps_U[:, q, l * T:(l + 1) * T],
                                                ctx_in[0:rows(c), q, c, l * P:(l + 1) * P],
                                                prob[0:rows(c), q, c * T:(c + 1) * T], start=(c == 0), stop=(c == MC - 1))
                last.then_inc(U_done, 1)

            def weight_sum(b, q):
                pe.wait_ge(probsum_set, b + 1)
                if not (isinstance(b, int) and b == 0):
                    pe.wait_ge(wsum_set, b)
                nc.tensor.matmul(ps_w[0:T, 0:1], probsum[0:MP, q, :], ones[0:MP, 0:1], start=True, stop=True).then_inc(wsum_done, 1)

            def values(b, q):
                pe.wait_ge(Uhi_set, b + 1)
                pe.wait_ge(Ulo_set, b + 1)
                if not first_two(b):
                    pe.wait_ge(y_set, b - 1)
                n = 0
                for upart, vpart in ((U_hi, Wv_hi), (U_hi, Wv_lo), (U_lo, Wv_hi)):
                    for l in range(LC):
                        last = nc.tensor.matmul(ps_Y[0:T, q, :], upart[:, q, l * T:(l + 1) * T], vpart[:, l, :],
                                                start=(n == 0), stop=(n == 3 * LC - 1))
                        n += 1
                last.then_inc(Y_done, 1)

            def turn(b, q):
                if exists(b):
                    scores_of(b, q)
                if exists(b - 3):
                    values(b - 3, 1 - q)
                if exists(b - 2):
                    weighted_ctx(b - 2, q)
                    weight_sum(b - 2, q)

            project(0)
            pe.wait_ge(wkq_step, EC)
            for c in range(LC):
                last = nc.tensor.matmul(ps_w[:, c:c + 1], wkq[:, (EC - 1) % 2, c * P:(c + 1) * P], ones[:, 0:1],
                                        start=True, stop=True)
            last.then_inc(gbias_summed, 1)
            project(1)
            scores_of(0, 0)
            sum_shift(0)
            project(2)
            scores_of(1, 1)
            sum_shift(1)
            project(3)
            sum_shift(2)
            turn(2, 0)
            sum_shift(3)
            pe.wait_ge(Wvhi_set, 1)
            pe.wait_ge(Wvlo_set, 1)
            each_turn(pe, turn, 3)
            weighted_ctx(B - 2, 0)
            weight_sum(B - 2, 0)
            values(B - 3, 1)
            values(B - 2, 0)
            weight_sum(B - 1, 1)
            pe.wait_ge(ctx_loaded[1], 16 * (B - 2) + 32)
            pe.wait_ge(prob_set, B)
            for l in range(LC):
                pe.wait_ge(Ulo_set, B - 2 if l == 0 else B - 1)
                for c in range(MC):
                    last = nc.tensor.matmul(ps_U[:, 1 - l, l * T:(l + 1) * T],
                                            ctx_in[0:rows(c), 1, c, l * P:(l + 1) * P],
                                            prob[0:rows(c), 1, c * T:(c + 1) * T], start=(c == 0), stop=(c == MC - 1))
                last.then_inc(last_U_done, 1)
            pe.wait_ge(y_set, B - 2)
            for l in range(LC):
                for upart, vpart in ((U_hi, Wv_hi), (U_hi, Wv_lo), (U_lo, Wv_hi)):
                    if upart is U_lo:
                        pe.wait_ge(last_Ulo_set, l + 1)
                    else:
                        pe.wait_ge(last_Uhi_set, l + 1)
                    last = nc.tensor.matmul(ps_Y[0:T, 1, :], upart[:, 1, l * T:(l + 1) * T], vpart[:, l, :],
                                            start=(l == 0 and upart is U_hi and vpart is Wv_hi),
                                            stop=(l == LC - 1 and upart is U_lo))
            last.then_inc(Y_done, 1)

        @block.scalar
        def _(act):
            with nc.allow_non_contiguous_dma("small constants"):
                act.dma_start(bk_in[:, :], bk.rearrange("(p c) -> p c", c=EC)).then_inc(bk_loaded, 16)
                act.dma_start(bq_col[:, :], bq.rearrange("(p c) -> p c", c=EC)).then_inc(bq_loaded, 16)

            def upper_half(g):
                q = g % 2
                if g >= 2:
                    act.wait_ge(G_summed, g - 1)
                for h in range(2):
                    act.wait_ge(xT_loaded[g][h], 16)
                    nc.scalar.activation(xT_hi[:, q, h * EH:(h + 1) * EH, :], xT_in[:, g % NX, h * EH:(h + 1) * EH, :],
                                         ACT.Copy).then_inc(xThi_set, 1)

            def take_group(g):
                bank = ps_Y if g % 2 == 0 else ps_U
                act.wait_ge(G_summed, g + 1)
                for c in range(LC):
                    last = nc.scalar.activation(G[:, c, g * GT:(g + 1) * GT], bank[:, c, 0:GT], ACT.Identity,
                                                bias=g_bias[:, c:c + 1])
                last.then_inc(G_set, 1)

            def upper_shift(g):
                act.wait_ge(xu_step, EC * (g + 1))
                if g >= 2:
                    act.wait_ge(c_summed, g - 1)
                nc.scalar.activation(xu_hi[:, g % 2, :], xu[:, (EC - 1) % 2, :], ACT.Copy).then_inc(xuhi_set, 1)

            def take_shift(g):
                act.wait_ge(c_summed, g + 1)
                nc.scalar.activation(c_rows[:, g * GT:(g + 1) * GT], ps_c[:, 0:GT], ACT.Copy).then_inc(c_set, 1)

            def exponentials(b, q):
                act.wait_ge(negmax_set, b + 1)
                if not first_two(b):
                    act.wait_ge(prob_set, b - 1)
                for c in range(MC):
                    last = nc.scalar.activation(expo[0:MP, q, c * T:(c + 1) * T], scores[0:MP, q, c * T:(c + 1) * T],
                                                ACT.Exp, bias=negmax[0:MP, q, c:c + 1],
                                                accum_out=expsum[0:MP, q, c:c + 1])
                last.then_inc(exp_done, 1)

            def upper_U(b, q):
                act.wait_ge(U_done, b + 1)
                if not first_two(b):
                    act.wait_ge(Y_done, b - 1)
                nc.scalar.activation(U_hi[:, q, :], ps_U[:, q, 0:LC * T], ACT.Copy).then_inc(Uhi_set, 1)

            def value_bias(b, q):
                act.wait_ge(wsum_done, b + 1)
                nc.scalar.activation(wsum[:, q:q + 1], ps_w[0:T, 0:1], ACT.Copy).then_inc(wsum_set, 1)
                act.wait_ge(wsum_set, b + 1)
                if not first_two(b):
                    act.wait_ge(resid_set, b - 1)
                nc.scalar.activation(bvw[:, q, :], bv_rows[:, :], ACT.Copy, scale=wsum[:, q:q + 1]).then_inc(bvw_set, 1)

            def scale_rows(b, q):
                act.wait_ge(centred_set, b + 1)
                act.wait_ge(rstd_set, b + 1)
                if not first_two(b):
                    act.wait_ge(result_set, b - 1)
                nc.scalar.activation(scaled[:, q, :], centred[:, q, :], ACT.Copy, scale=rstd[:, q:q + 1]).then_inc(scaled_set, 1)

            def store(b, q):
                act.wait_ge(result_set, b + 1)
                act.dma_start(out[b, :, :], result[:, q, :]).then_inc(out_stored[q], 16)

            def turn(b, q):
                if exists(b - 3):
                    upper_U(b - 3, 1 - q)
                    value_bias(b - 3, 1 - q)
                if exists(b - 4):
                    scale_rows(b - 4, q)
                if exists(b):
                    exponentials(b, q)
                    if exists(b - 4):
                        store(b - 4, q)

            banks = [ps_S[:, 0, :], ps_S[:, 1, :], ps_U[:, 0, :], ps_U[:, 1, :]]
            act.wait_ge(consts_set, 1)
            nc.scalar.activation(ones_r[:, :], ones[:, :], ACT.Copy).then_inc(onesr_set, 1)
            for f in range(EC):
                act.wait_ge(w_in[f], 32)
                nc.scalar.activation(wq_hi[:, f, :], wqT[:, f, :], ACT.Copy).then_inc(wqhi_set, 1)
            upper_half(0)
            for e in range(EC):
                act.wait_ge(W_summed, e + 1)
                nc.scalar.activation(W_hi[:, e, :], banks[e][:, 0:L], ACT.Copy, scale=SCALE).then_inc(Whi_set, 1)
            upper_half(1)
            act.wait_ge(gbias_summed, 1)
            nc.scalar.activation(g_bias[:, :], ps_w[:, 0:LC], ACT.Copy, scale=SCALE).then_inc(gbias_set, 1)
            act.wait_ge(gbias_set, 1)
            take_group(0)
            upper_shift(0)
            upper_half(2)
            take_group(1)
            upper_half(3)
            upper_shift(1)
            take_shift(0)
            exponentials(0, 0)
            take_group(2)
            upper_shift(2)
            act.wait_ge(wv_loaded, 16)
            nc.scalar.activation(Wv_hi[:, :, :], wv_in[:, :, :], ACT.Copy).then_inc(Wvhi_set, 1)
            take_shift(1)
            exponentials(1, 1)
            take_group(3)
            take_shift(2)
            upper_shift(3)
            act.wait_ge(rows_in, 48)
            upper_U(0, 0)
            exponentials(2, 0)
            take_shift(3)
            value_bias(0, 0)
            exponentials(3, 1)
            each_turn(act, turn, 4)
            upper_U(B - 3, 1)
            value_bias(B - 3, 1)
            scale_rows(B - 4, 0)
            upper_U(B - 2, 0)
            value_bias(B - 2, 0)
            value_bias(B - 1, 1)
            act.wait_ge(Y_done, B - 2)
            for l in range(LC):
                act.wait_ge(last_U_done, l + 1)
                nc.scalar.activation(U_hi[:, 1, l * T:(l + 1) * T], ps_U[:, 1 - l, l * T:(l + 1) * T],
                                     ACT.Copy).then_inc(last_Uhi_set, 1)
                scale_rows(B - 3 + l, 1 - l)

        @block.vector
        def _(dve):
            nc.vector.memset(ones[:, :], 1.0).then_inc(consts_set, 1)
            nc.vector.memset(neg_half[:, :], -0.5).then_inc(consts_set, 1)
            dve.wait_ge(bk_loaded, 16)
            nc.vector.tensor_copy(wkT[:, :, L:L + 2], bk_in[:, :].unsqueeze(2).to_broadcast([P, EC, 2])).then_inc(bkcol_set, 1)
            dve.wait_ge(bkcol_set, 1)
            for c in range(EC):
                dve.wait_ge(w_in[c], 32)
                nc.vector.tensor_copy(wk_hi[:, c, :], wkT[:, c, :]).then_inc(wkhi_set, 1)
                dve.wait_ge(wqhi_set, c + 1)
                nc.vector.tensor_tensor(wq_lo[:, c, :], wqT[:, c, :], wq_hi[:, c, :].bitcast(F32), ALU.subtract).then_inc(wqlo_set, 1)
                if c == 0:
                    dve.wait_ge(bq_loaded, 16)
                    nc.vector.tensor_scalar(wkq[:, 0, :], wkT[:, 0, :], bq_col[:, 0:1], None, ALU.mult).then_inc(wkq_step, 1)
                else:
                    dve.wait_ge(wkq_step, c)
                    nc.vector.scalar_tensor_tensor(wkq[:, c % 2, :], wkT[:, c, :], bq_col[:, c:c + 1],
                                                   wkq[:, (c - 1) % 2, :], ALU.mult, ALU.add).then_inc(wkq_step, 1)

            banks = [ps_S[:, 0, :], ps_S[:, 1, :], ps_U[:, 0, :], ps_U[:, 1, :]]
            def lower_half(g):
                q = g % 2
                for h in range(2):
                    dve.wait_ge(xThi_set, 2 * g + h + 1)
                    nc.vector.tensor_tensor(xT_lo[:, q, h * EH:(h + 1) * EH, :], xT_in[:, g % NX, h * EH:(h + 1) * EH, :],
                                            xT_hi[:, q, h * EH:(h + 1) * EH, :].bitcast(F32),
                                            ALU.subtract).then_inc(xTlo_set, 1)

            def weigh_by_u(g):
                q = g % 2
                if g >= 1:
                    dve.wait_ge(xulo_set, g)
                nc.vector.tensor_scalar(xu[:, 0, :], xT_in[:, g % NX, 0, :], u_col[:, 0:1], bb_col[:, 0:1],
                                        ALU.mult, ALU.add).then_inc(xu_step, 1)
                for e in range(1, EC):
                    dve.wait_ge(xu_step, EC * g + e)
                    nc.vector.scalar_tensor_tensor(xu[:, e % 2, :], xT_in[:, g % NX, e, :], u_col[:, e:e + 1],
                                                   xu[:, (e - 1) % 2, :], ALU.mult, ALU.add).then_inc(xu_step, 1)

            def lower_shift(g):
                dve.wait_ge(xuhi_set, g + 1)
                if g >= 2:
                    dve.wait_ge(c_summed, g - 1)
                nc.vector.tensor_tensor(xu_lo[:, g % 2, :], xu[:, (EC - 1) % 2, :],
                                        xu_hi[:, g % 2, :].bitcast(F32), ALU.subtract).then_inc(xulo_set, 1)

            def maxima(b, q):
                if isinstance(b, int):
                    dve.wait_ge(c_set, NG if b == FIRST - 1 else b // GB + 1)
                dve.wait_ge(S_done, b + 1)
                if not first_two(b):
                    dve.wait_ge(exp_done, b - 1)
                shift = c_rows[0:MP, bass.ds(b * T, T)].unsqueeze(1).unsqueeze(1).to_broadcast([MP, 2, HALF, T])
                nc.vector.tensor_tensor(split_chunks(scores[0:MP, q, :]),
                                        ps_S[0:MP, :, 0:HALF * T].rearrange("p b (c t) -> p b c t", t=T),
                                        shift, ALU.add).then_inc(S_read, 1)
                dve.wait_ge(S_read, b + 1)
                nc.vector.tensor_reduce(negmax[0:MP, q, :], scores[0:MP, q, :].rearrange("p (c t) -> p c t", t=T),
                                        AX.X, ALU.max, negate=True).then_inc(negmax_set, 1)

            def normaliser(b, q):
                dve.wait_ge(exp_done, b + 1)
                nc.vector.reciprocal(rall[0:MP, q, :], expsum[0:MP, q, :]).then_inc(rall_set, 1)
                dve.wait_ge(rall_set, b + 1)
                nc.vector.tensor_tensor(rinv[0:MP, q, :], rall[0:MP, q, :], mask[0:MP, :], ALU.mult).then_inc(rinv_set, 1)

            def chunk_sum(b, q):
                dve.wait_ge(prob_set, b + 1)
                if not first_two(b):
                    dve.wait_ge(wsum_done, b - 1)
                nc.vector.tensor_reduce(probsum[0:MP, q, :], prob[0:MP, q, :].rearrange("p (c t) -> p t c", t=T),
                                        AX.X, ALU.add).then_inc(probsum_set, 1)

            def lower_U(b, q):
                dve.wait_ge(Uhi_set, b + 1)
                nc.vector.tensor_tensor(U_lo[:, q, :], ps_U[:, q, 0:LC * T], U_hi[:, q, :].bitcast(F32),
                                        ALU.subtract).then_inc(Ulo_set, 1)

            def add_residual(b, q):
                dve.wait_ge(Y_done, b + 1)
                dve.wait_ge(resid_set, b + 1)
                nc.vector.tensor_tensor(y[:, q, :], ps_Y[0:T, q, :], resid[:, q, :], ALU.add).then_inc(y_set, 1)

            def row_stats(b, q):
                dve.wait_ge(y_set, b + 1)
                nc.vector.bn_stats(stats[:, q, :], y[:, q, :]).then_inc(stats_set, 1)
                dve.wait_ge(stats_set, b + 1)

            def aggregate(b, q):
                nc.vector.bn_aggr(meanvar[:, q, :], stats[:, q, :]).then_inc(meanvar_set, 1)
                dve.wait_ge(meanvar_set, b + 1)
                if not first_two(b):
                    dve.wait_ge(scaled_set, b - 1)
                nc.vector.tensor_scalar(vareps[:, q:q + 1], meanvar[:, q, 1:2], EPS, None, ALU.add).then_inc(vareps_set, 1)

            def centred_rows(b, q):
                nc.vector.scalar_tensor_tensor(centred[:, q, :], y[:, q, :], meanvar[:, q, 0:1], gamma_rows[:, :],
                                               ALU.subtract, ALU.mult).then_inc(centred_set, 1)

            def centre(b, q):
                aggregate(b, q)
                centred_rows(b, q)

            def turn(b, q):
                if exists(b - 1):
                    normaliser(b - 1, 1 - q)
                if exists(b - 3):
                    lower_U(b - 3, 1 - q)
                if exists(b):
                    maxima(b, q)
                if exists(b - 3):
                    add_residual(b - 3, 1 - q)
                    row_stats(b - 3, 1 - q)
                if exists(b - 1):
                    chunk_sum(b - 1, 1 - q)
                if exists(b - 3):
                    centre(b - 3, 1 - q)

            lower_half(0)
            for e in range(EC):
                dve.wait_ge(Whi_set, e + 1)
                nc.vector.scalar_tensor_tensor(W_lo[:, e, :], banks[e][:, 0:L], SCALE, W_hi[:, e, :].bitcast(F32),
                                               ALU.mult, ALU.subtract).then_inc(Wlo_set, 1)
            for e in range(EC):
                nc.vector.tensor_scalar(u_col[:, e:e + 1], banks[e][:, L:L + 1], SCALE, None, ALU.mult).then_inc(u_set, 1)
            lower_half(1)
            dve.wait_ge(wkq_step, EC)
            nc.vector.tensor_scalar(bb_col[:, :], wkq[:, (EC - 1) % 2, L:L + 1], SCALE, None, ALU.mult).then_inc(bb_set, 1)
            dve.wait_ge(bb_set, 1)
            dve.wait_ge(u_set, EC)
            nc.vector.memset(ps_scores(MC - 1), 0.0).then_inc(scores_zeroed, 1)
            weigh_by_u(0)
            lower_shift(0)
            weigh_by_u(1)
            dve.wait_ge(mask_set, 2)
            dve.wait_ge(scores_zeroed, 1)
            maxima(0, 0)
            lower_shift(1)
            weigh_by_u(2)
            normaliser(0, 0)
            maxima(1, 1)
            chunk_sum(0, 0)
            lower_shift(2)
            weigh_by_u(3)
            dve.wait_ge(rows_in, 48)
            lower_shift(3)
            normaliser(1, 1)
            maxima(2, 0)
            lower_U(0, 0)
            chunk_sum(1, 1)
            normaliser(2, 0)
            maxima(3, 1)
            add_residual(0, 0)
            row_stats(0, 0)
            chunk_sum(2, 0)
            centre(0, 0)
            each_turn(dve, turn, 4)
            normaliser(B - 1, 1)
            lower_U(B - 3, 1)
            lower_U(B - 2, 0)
            chunk_sum(B - 1, 1)
            add_residual(B - 3, 1)
            row_stats(B - 3, 1)
            centre(B - 3, 1)
            add_residual(B - 2, 0)
            for l in range(LC):
                dve.wait_ge(last_Uhi_set, l + 1)
                nc.vector.tensor_tensor(U_lo[:, 1, l * T:(l + 1) * T], ps_U[:, 1 - l, l * T:(l + 1) * T],
                                        U_hi[:, 1, l * T:(l + 1) * T].bitcast(F32),
                                        ALU.subtract).then_inc(last_Ulo_set, 1)
                if l == 0:
                    row_stats(B - 2, 0)
                    aggregate(B - 2, 0)
            centred_rows(B - 2, 0)
            add_residual(B - 1, 1)
            row_stats(B - 1, 1)
            centre(B - 1, 1)
            dve.wait_ge(rstd_set, B)
            dve.wait_ge(centred_set, B)
            dve.wait_ge(result_set, B - 2)
            nc.vector.scalar_tensor_tensor(scaled[:, 1, :], centred[:, 1, :], rstd[:, 1:2], beta_rows[:, :],
                                           ALU.mult, ALU.add).then_inc(result_set, 1)

        @block.gpsimd
        def _(pool):
            pool.wait_ge(bkcol_set, 1)
            for c in range(EC):
                pool.wait_ge(w_in[c], 32)
                pool.wait_ge(wkhi_set, c + 1)
                nc.gpsimd.tensor_tensor(wk_lo[:, c, :], wkT[:, c, :], wk_hi[:, c, :].bitcast(F32), ALU.subtract).then_inc(wklo_set, 1)
            nc.gpsimd.memset(mask[:, :], 1.0).then_inc(mask_set, 1)
            pool.wait_ge(mask_set, 1)
            nc.gpsimd.affine_select(out=mask[:, MC - 1:MC], in_=mask[:, MC - 1:MC], compare_op=ALU.is_ge, fill=0.0,
                                    base=ML - 1, pattern=[[0, 1]], channel_multiplier=-1).then_inc(mask_set, 1)

            def probabilities(b, q):
                pool.wait_ge(rinv_set, b + 1)
                if not first_two(b):
                    pool.wait_ge(U_done, b - 1)
                    pool.wait_ge(probsum_set, b - 1)
                nc.gpsimd.tensor_tensor(prob[0:MP, q, :].rearrange("p (c t) -> p c t", t=T),
                                        expo[0:MP, q, :].rearrange("p (c t) -> p c t", t=T),
                                        rinv[0:MP, q, :].unsqueeze(2).to_broadcast([MP, MC, T]),
                                        ALU.mult).then_inc(prob_set, 1)

            def residual(b, q):
                pool.wait_ge(x_loaded[q], 8 * (b - q) + 16)
                pool.wait_ge(bvw_set, b + 1)
                if not first_two(b):
                    pool.wait_ge(y_set, b - 1)
                nc.gpsimd.tensor_tensor(resid[:, q, :], x_in[:, q, :], bvw[:, q, :], ALU.add).then_inc(resid_set, 1)

            def inverse_deviation(b, q):
                pool.wait_ge(vareps_set, b + 1)
                nc.gpsimd.tensor_tensor(rstd[:, q:q + 1], vareps[:, q:q + 1], neg_half[:, :], ALU.pow).then_inc(rstd_set, 1)

            def finish(b, q):
                pool.wait_ge(scaled_set, b + 1)
                if not first_two(b):
                    pool.wait_ge(out_stored[q], 8 * (b - q))
                nc.gpsimd.tensor_tensor(result[:, q, :], scaled[:, q, :], beta_rows[:, :], ALU.add).then_inc(result_set, 1)

            def lower_half(g):
                q = g % 2
                pool.wait_ge(G_summed, g - 1)
                for h in range(2):
                    pool.wait_ge(xThi_set, 2 * g + h + 1)
                    nc.gpsimd.tensor_tensor(xT_lo[:, q, h * EH:(h + 1) * EH, :], xT_in[:, g % NX, h * EH:(h + 1) * EH, :],
                                            xT_hi[:, q, h * EH:(h + 1) * EH, :].bitcast(F32),
                                            ALU.subtract).then_inc(xTlo_set, 1)

            def turn(b, q):
                if exists(b - 4):
                    inverse_deviation(b - 4, q)
                if exists(b - 3):
                    residual(b - 3, 1 - q)
                if exists(b - 4):
                    finish(b - 4, q)
                if exists(b - 1):
                    probabilities(b - 1, 1 - q)

            pool.wait_ge(mask_set, 2)
            pool.wait_ge(consts_set, 2)
            lower_half(2)
            lower_half(3)
            turn(1, 1)
            pool.wait_ge(Wvhi_set, 1)
            nc.gpsimd.tensor_tensor(Wv_lo[:, :, :], wv_in[:, :, :], Wv_hi[:, :, :].bitcast(F32),
                                    ALU.subtract).then_inc(Wvlo_set, 1)
            pool.wait_ge(rows_in, 48)
            each_turn(pool, turn, 2)
            inverse_deviation(B - 4, 0)
            residual(B - 3, 1)
            probabilities(B - 1, 1)
            residual(B - 2, 0)
            finish(B - 4, 0)
            inverse_deviation(B - 3, 1)
            residual(B - 1, 1)
            inverse_deviation(B - 2, 0)
            finish(B - 3, 1)
            finish(B - 2, 0)
            inverse_deviation(B - 1, 1)


def kernel(x, ctx_512, L0_xattn_Wq, L0_xattn_bq, L0_xattn_Wk, L0_xattn_bk, L0_xattn_Wv, L0_xattn_bv,
           L0_xattn_gamma, L0_xattn_beta):
    import numpy as np
    import concourse.bacc as bacc
    from concourse.bass_utils import run_bass_kernel_spmd

    x = np.asarray(x)
    ctx = np.asarray(ctx_512)
    B, T, E = x.shape
    groups = 4
    arrays = {
        "xT": np.ascontiguousarray(x.reshape(groups, B // groups * T, E).transpose(0, 2, 1)),
        "x": np.ascontiguousarray(x),
        "ctxT": np.ascontiguousarray(ctx.transpose(0, 2, 1)),
        "ctx": np.ascontiguousarray(ctx),
        "WqT": np.ascontiguousarray(np.asarray(L0_xattn_Wq).T),
        "WkT": np.ascontiguousarray(np.asarray(L0_xattn_Wk).T),
        "bq": np.asarray(L0_xattn_bq),
        "bk": np.asarray(L0_xattn_bk),
        "Wv": np.asarray(L0_xattn_Wv),
        "bv": np.asarray(L0_xattn_bv),
        "gamma": np.asarray(L0_xattn_gamma),
        "beta": np.asarray(L0_xattn_beta),
    }
    nc = bacc.Bacc("TRN2", target_bir_lowering=False, num_devices=1)
    args = [nc.dram_tensor(n, a.shape, F32, kind="ExternalInput").ap() for n, a in arrays.items()]
    out = nc.dram_tensor("out", x.shape, F32, kind="ExternalOutput").ap()
    xattn(nc, *args, out)
    return run_bass_kernel_spmd(nc, [arrays], core_ids=[0]).results[0]["out"]
```
